# Optimizing a Trainium2 kernel written in Bass

```python
import numpy as np
import jax
import jax.numpy as jnp

def _softmax(x, axis=-1):
    return jax.nn.softmax(x, axis=axis)

def _gelu(x):
    return jax.nn.gelu(x, approximate=True)

def _silu(x):
    return jax.nn.silu(x)

def _sigmoid(x):
    return jax.nn.sigmoid(x)

def _layernorm(x, axis=-1, eps=1e-05):
    m = jnp.mean(x, axis=axis, keepdims=True)
    v = jnp.var(x, axis=axis, keepdims=True)
    return (x - m) / jnp.sqrt(v + eps)

def _scatter_add(tgt, idx, src, axis=0):
    return tgt.at[idx].add(src)

def _segment_sum(src, seg, n):
    return jax.ops.segment_sum(src, seg, n)
kernel_name = 'mk_sandwich_d1_jaxref_r4_41892a'

def setup_inputs(seed: int=0):
    np.random.seed(seed)
    _w = jnp.asarray

    def _L0_attn_setup():
        import jax, jax.numpy as jnp
        import numpy as np
        B, T, C = (4, 512, 256)
        H, D = (16, 64)
        MAX_REL = 16
        NUM_BUCKETS = 2 * MAX_REL + 1
        key = jax.random.key(seed)
        ks = jax.random.split(key, 7)
        x = jax.random.normal(ks[0], (B, T, C), dtype=jnp.float32)
        Wq = jax.random.normal(ks[1], (H, C, D), dtype=jnp.float32) * 0.02
        Wk = jax.random.normal(ks[2], (H, C, D), dtype=jnp.float32) * 0.02
        Wv = jax.random.normal(ks[3], (H, C, D), dtype=jnp.float32) * 0.02
        Wp = jax.random.normal(ks[4], (H * D, C), dtype=jnp.float32) * 0.02
        bp = jnp.zeros((C,), dtype=jnp.float32)
        rel_table = jax.random.normal(ks[5], (NUM_BUCKETS, H), dtype=jnp.float32) * 0.02
        return {'x': x, 'Wq': Wq, 'Wk': Wk, 'Wv': Wv, 'Wp': Wp, 'bp': bp, 'rel_table': rel_table}
    _L0_attn_in = _L0_attn_setup()

    def _L0_ffn_setup():
        import jax, jax.numpy as jnp
        import numpy as np
        DIM = 256

        def _reference_tuple_inner(x, W_r, W_k, W_v, mu_r, mu_k):
            B, T, C = x.shape
            x_prev = jnp.concatenate([jnp.zeros((B, 1, C), x.dtype), x[:, :-1, :]], axis=1)
            xr = mu_r * x + (1.0 - mu_r) * x_prev
            xk = mu_k * x + (1.0 - mu_k) * x_prev
            r = jax.nn.sigmoid(jnp.einsum('btc,dc->btd', xr, W_r))
            k = jnp.einsum('btc,dc->btd', xk, W_k)
            k_act = jnp.square(jax.nn.relu(k))
            out = r * jnp.einsum('btc,dc->btd', k_act, W_v)
            new_state = x[:, -1, :]
            return (out, new_state)
        key = jax.random.key(seed)
        ks = jax.random.split(key, 6)
        B, T, C = (8, 512, DIM)
        x = jax.random.normal(ks[0], (B, T, C), dtype=jnp.float32)
        s = 1.0 / np.sqrt(C)
        W_r = jax.random.uniform(ks[1], (C, C), jnp.float32, -s, s)
        W_k = jax.random.uniform(ks[2], (C, C), jnp.float32, -s, s)
        W_v = jax.random.uniform(ks[3], (C, C), jnp.float32, -s, s)
        mu_r = jax.random.uniform(ks[4], (C,), jnp.float32)
        mu_k = jax.random.uniform(ks[5], (C,), jnp.float32)
        return {'x': x, 'W_r': W_r, 'W_k': W_k, 'W_v': W_v, 'mu_r': mu_r, 'mu_k': mu_k}
    _L0_ffn_in = _L0_ffn_setup()
    _d = {'L0_attn_x': _L0_attn_in['x'], 'L0_attn_Wq': _L0_attn_in['Wq'], 'L0_attn_Wk': _L0_attn_in['Wk'], 'L0_attn_Wv': _L0_attn_in['Wv'], 'L0_attn_Wp': _L0_attn_in['Wp'], 'L0_attn_bp': _L0_attn_in['bp'], 'L0_attn_rel_table': _L0_attn_in['rel_table'], 'L0_ffn_W_r': _L0_ffn_in['W_r'], 'L0_ffn_W_k': _L0_ffn_in['W_k'], 'L0_ffn_W_v': _L0_ffn_in['W_v'], 'L0_ffn_mu_r': _L0_ffn_in['mu_r'], 'L0_ffn_mu_k': _L0_ffn_in['mu_k']}
    _x0 = _d['L0_attn_x']
    _d['L0_attn_x'] = jax.random.normal(jax.random.fold_in(jax.random.key(seed), 1), (8, 1024, 256), dtype=_x0.dtype)
    del _x0
    return _d

def reference(L0_attn_x, L0_attn_Wq, L0_attn_Wk, L0_attn_Wv, L0_attn_Wp, L0_attn_bp, L0_attn_rel_table, L0_ffn_W_r, L0_ffn_W_k, L0_ffn_W_v, L0_ffn_mu_r, L0_ffn_mu_k):

    def _L0_attn_ref(x, Wq, Wk, Wv, Wp, bp, rel_table):
        import jax, jax.numpy as jnp
        import numpy as np
        B, T, C = (4, 512, 256)
        H, D = (16, 64)
        MAX_REL = 16
        NUM_BUCKETS = 2 * MAX_REL + 1
        Tq = x.shape[1]
        pos = jnp.arange(Tq)
        rel = pos[None, :] - pos[:, None]
        idx = jnp.clip(rel + MAX_REL, 0, NUM_BUCKETS - 1)
        bias = rel_table[idx]
        bias = jnp.transpose(bias, (2, 0, 1))
        q = jnp.einsum('btc,hcd->bhtd', x, Wq)
        k = jnp.einsum('btc,hcd->bhtd', x, Wk)
        v = jnp.einsum('btc,hcd->bhtd', x, Wv)
        scale = 1.0 / jnp.sqrt(jnp.float32(D))
        scores = jnp.einsum('bhtd,bhsd->bhts', q, k) * scale + bias[None]
        causal = jnp.tril(jnp.ones((Tq, Tq), dtype=bool))
        scores = jnp.where(causal[None, None], scores, jnp.float32(-jnp.inf))
        w = jax.nn.softmax(scores, axis=-1)
        out = jnp.einsum('bhts,bhsd->bhtd', w, v)
        out = jnp.transpose(out, (0, 2, 1, 3)).reshape(x.shape[0], Tq, H * D)
        return out @ Wp + bp

    def _L0_ffn_ref(x, W_r, W_k, W_v, mu_r, mu_k):
        import jax, jax.numpy as jnp
        import numpy as np
        DIM = 256

        def _reference_tuple_inner(x, W_r, W_k, W_v, mu_r, mu_k):
            B, T, C = x.shape
            x_prev = jnp.concatenate([jnp.zeros((B, 1, C), x.dtype), x[:, :-1, :]], axis=1)
            xr = mu_r * x + (1.0 - mu_r) * x_prev
            xk = mu_k * x + (1.0 - mu_k) * x_prev
            r = jax.nn.sigmoid(jnp.einsum('btc,dc->btd', xr, W_r))
            k = jnp.einsum('btc,dc->btd', xk, W_k)
            k_act = jnp.square(jax.nn.relu(k))
            out = r * jnp.einsum('btc,dc->btd', k_act, W_v)
            new_state = x[:, -1, :]
            return (out, new_state)
        return _reference_tuple_inner(x, W_r, W_k, W_v, mu_r, mu_k)[0]
    x = L0_attn_x
    x = x + _layernorm(_L0_attn_ref(_layernorm(x, axis=-1), L0_attn_Wq, L0_attn_Wk, L0_attn_Wv, L0_attn_Wp, L0_attn_bp, L0_attn_rel_table), axis=-1)
    x = x + _layernorm(_L0_ffn_ref(_layernorm(x, axis=-1), L0_ffn_W_r, L0_ffn_W_k, L0_ffn_W_v, L0_ffn_mu_r, L0_ffn_mu_k), axis=-1)
    return x

_drawn_inputs = setup_inputs


def setup_inputs(seed=0):
    import zlib

    import numpy as np

    out = dict(_drawn_inputs(seed))
    spreads = {'L0_attn_bp': (0.0, 0.1)}
    factors = {'L0_attn_Wq': 3.981, 'L0_attn_Wk': 3.997, 'L0_attn_rel_table': 24.807}
    for name, (base, spread) in spreads.items():
        noise = np.random.default_rng([zlib.crc32(name.encode()), seed]).standard_normal(out[name].shape)
        drawn = base * np.exp(spread * noise) if base else spread * noise
        out[name] = jnp.asarray(drawn.astype(out[name].dtype))
    for name, factor in factors.items():
        out[name] = (out[name] * factor).astype(out[name].dtype)
    return out
```

```python
from contextlib import ExitStack
from math import log

import concourse.bass as bass
from concourse import mybir

P = 128
B, T, C, H, D = 8, 1024, 256, 16, 64
NBUCKET, MAX_REL = 33, 16
KT = C // P
NB = T // P
NPAIR = H // 2
N = B * NPAIR
G = B * NB
UNITS = 2 * NB
HEAD_LEAD, TAIL_LAG = NB + 1, NPAIR + 1
RING = 2 * T
WIN = P + MAX_REL
ROW = WIN + P
MASKED = -3.0e38
EPS = 1e-5
W_TOP = 64.0
P_SHIFT = 14 * log(2.0)
RSQRT_SEED = float(0x5F3759DF)
NEWTON = 3
LN_OPS = 2 + 3 * NEWTON

ALU = mybir.AluOpType
ACT = mybir.ActivationFunctionType
AX = mybir.AxisListType
F32, F16, I32 = mybir.dt.float32, mybir.dt.float16, mybir.dt.int32

NEXT_TASKS = {"q0": 0, "q1": 1, "k0": 2, "k1": 3, "v0": 8, "v1": 9}
TAIL_TASKS = {"ot0": 4, "ot1": 5, "proj": 6, "x2t": 11, "rk": 13, "ffn": 15}
HEAD_TASKS = {"xt": 12}


class Segment:

    def __init__(self, lo, hi, base):
        self.lo, self.hi, self.base = lo, hi, base
        self.next = lo < N - 1
        self.head = lo < G - HEAD_LEAD
        self.tail = lo >= TAIL_LAG
        slots = {**(NEXT_TASKS if self.next else {}), **(TAIL_TASKS if self.tail else {}),
                 **(HEAD_TASKS if self.head else {})}
        self.order = sorted(slots, key=slots.get)
        self.in_slot = {slots[name]: name for name in self.order}
        self.end_base = base + len(self.order) * (hi - lo)

    def index(self, n, name):
        return self.base + len(self.order) * (n - self.lo) + self.order.index(name)


def plan():
    segments, base = [], HEAD_LEAD + len(NEXT_TASKS)
    for lo, hi in ((0, 1), (1, TAIL_LAG), (TAIL_LAG, TAIL_LAG + 1), (TAIL_LAG + 1, G - HEAD_LEAD), (G - HEAD_LEAD, N - 1), (N - 1, N)):
        segments.append(Segment(lo, hi, base))
        base = segments[-1].end_base
    return segments, base


def chunks(i):
    return [(c, min(4, i + 1 - 4 * c)) for c in range((i + 4) // 4)]


CHUNK0 = [sum(len(chunks(k % NB)) for k in range(u)) for u in range(UNITS + 1)]
CHUNKS = CHUNK0[UNITS]


def chunks_before(u):
    return CHUNKS * (u // UNITS) + CHUNK0[u % UNITS]


def build(nc, x, wqkv, wp, bp, table, w_r, w_k, w_v, mu_r, mu_k, out):
    segments, tail_base = plan()
    with ExitStack() as ctx:
        def sb(name, shape, dt):
            return ctx.enter_context(nc.sbuf_tensor(name, shape, dt))

        def ps(name, shape):
            return ctx.enter_context(nc.psum_tensor(name, shape, F32))

        def sem(name):
            return ctx.enter_context(nc.semaphore(name))

        o_dram = nc.dram_tensor("o_scratch", [B * T, H * D], F32, kind="Internal").ap()
        band_dram = nc.dram_tensor("band_scratch", [H, P * ROW], F32, kind="Internal").ap()

        ident = sb("ident", [P, P], F32)
        w_f32 = sb("w_f32", [P, 3, KT, H * D], F32)
        w_split = sb("w_split", [P, 2, 3, KT, H * D], F16)
        wp_sb = sb("wp_sb", [P, H * D // P, C], F32)
        wr_sb = sb("wr_sb", [P, KT, C], F32)
        wk_sb = sb("wk_sb", [P, KT, C], F32)
        wv_sb = sb("wv_sb", [P, KT, C], F32)
        bp_sb = sb("bp_sb", [P, C], F32)
        mu_sb = sb("mu_sb", [P, 2, KT], F32)
        tab_sb = sb("tab_sb", [P, NBUCKET, H], F32)
        band_src = sb("band_src", [P, H, ROW], F32)
        band = sb("band", [P, H, WIN], F32)
        top = sb("top", [P, 3], F32)
        top_all = sb("top_all", [P, 3], F32)
        pow2 = sb("pow2", [P, 3], F32)
        inv2 = sb("inv2", [P, 3], F32)
        w_scale = sb("w_scale", [P, 3], F32)
        score_unit = sb("score_unit", [P, 1], F32)
        band_unit = sb("band_unit", [P, 1], F32)
        keep_carry = sb("keep_carry", [P, G], F32)

        xh = sb("xh", [P, C], F32)
        xh_norm = sb("xh_norm", [P, C], F32)
        xT = sb("xT", [P, 2, KT, RING], F16)

        q_stage = sb("q_stage", [P, 2, T], F16)
        k_stage = sb("k_stage", [P, 2, T], F16)
        v_stage = sb("v_stage", [P, NB, 2, 2, D], F16)
        q_pair = [sb(f"q_pair{h}", [P, T], F16) for h in range(2)]
        k_twice = [sb(f"k_twice{h}", [P, 2, T], F16) for h in range(2)]
        v_head = [sb(f"v_head{h}", [P, NB, 2 * D], F16) for h in range(2)]

        probs = sb("probs", [P, 2, T], F32)
        probsT = sb("probsT", [P, 2, 2, NB, P], F16)
        neg_max = sb("neg_max", [P, 4], F32)
        exp_bias = sb("exp_bias", [P, 4], F32)
        row_sum = sb("row_sum", [P, 4], F32)
        inv_sum = sb("inv_sum", [P, 4], F32)
        o_parts = sb("o_parts", [P, 2, 2 * D], F32)
        o_stage = [sb(f"o_stage{h}", [P, NB, D], F32) for h in range(2)]

        o_cur = sb("o_cur", [P, H * D], F32)
        oT = sb("oT", [P, H * D // P, P], F32)
        x_res = sb("x_res", [P, C], F32)
        y = sb("y", [P, C], F32)
        y_norm = sb("y_norm", [P, C], F32)
        x2 = sb("x2", [P, C], F32)
        x2_norm = sb("x2_norm", [P, C], F32)
        x2T = sb("x2T", [P, KT, P + 1], F32)
        delta = sb("delta", [P, KT, P], F32)
        mixed = sb("mixed", [P, 2, KT, P], F32)
        gate_exp = sb("gate_exp", [P, C], F32)
        gate_den = sb("gate_den", [P, C], F32)
        gate = sb("gate", [P, C], F32)
        k_relu = sb("k_relu", [P, KT, P], F32)
        k_act = sb("k_act", [P, KT, P], F32)
        z = sb("z", [P, C], F32)
        z_norm = sb("z_norm", [P, C], F32)
        out_sb = sb("out_sb", [P, C], F32)

        scores = ps("scores", [P, 2, T])
        probsT_ps = [ps(f"probsT_ps{k}", [P, 4, P]) for k in range(2)]
        o_ps = ps("o_ps", [P, 512])
        misc = ps("misc", [P, 512])

        weights_in, small_in = sem("weights_in"), sem("small_in")
        table_in, band_out, band_in = sem("table_in"), sem("band_out"), sem("band_in")
        pool_setup, top_ready, top_reduced = sem("pool_setup"), sem("top_ready"), sem("top_reduced")
        vec_setup, split_hi, split_lo = sem("vec_setup"), sem("split_hi"), sem("split_lo")
        ident_ready = sem("ident_ready")
        misc_full, misc_free, misc_hi = sem("misc_full"), sem("misc_free"), sem("misc_hi")
        xh_in, xh_stats, xh_aggr = sem("xh_in"), sem("xh_stats"), sem("xh_aggr")
        xh_pool, xh_ready = sem("xh_pool"), sem("xh_ready")
        qk_in = [sem(f"qk_in{h}") for h in range(2)]
        v_in = [sem(f"v_in{h}") for h in range(2)]
        o_stored = [sem(f"o_stored{h}") for h in range(2)]
        scored, band_added, max_ready = sem("scored"), sem("band_added"), sem("max_ready")
        bias_ready, exp_done, transposed = sem("bias_ready"), sem("exp_done"), sem("transposed")
        hi_done, lo_done, pv_done = sem("hi_done"), sem("lo_done"), sem("pv_done")
        inv_ready, parts_ready, o_added = sem("inv_ready"), sem("parts_ready"), sem("o_added")
        o_cur_in, x_res_in = sem("o_cur_in"), sem("x_res_in")
        y_ready, y_stats, y_aggr, y_pool, y_normed = (
            sem("y_ready"), sem("y_stats"), sem("y_aggr"), sem("y_pool"), sem("y_normed"))
        x2_ready, x2_stats, x2_aggr, x2_pool, x2_normed = (
            sem("x2_ready"), sem("x2_stats"), sem("x2_aggr"), sem("x2_pool"), sem("x2_normed"))
        carried, delta_ready, mixed_ready = sem("carried"), sem("delta_ready"), sem("mixed_ready")
        gate_exped, relued, den_ready, gate_ready, k_act_ready = (
            sem("gate_exped"), sem("relued"), sem("den_ready"), sem("gate_ready"), sem("k_act_ready"))
        z_ready, z_stats, z_aggr, z_pool, z_normed = (
            sem("z_ready"), sem("z_stats"), sem("z_aggr"), sem("z_pool"), sem("z_normed"))
        out_ready, out_stored = sem("out_ready"), sem("out_stored")

        ln_bufs = {}
        for name in ("xh", "y", "x2", "z"):
            ln_bufs[name] = (sb(f"{name}_bn", [P, 6], F32), sb(f"{name}_mv", [P, 2], F32),
                             sb(f"{name}_var", [P, 1], F32), sb(f"{name}_a", [P, 1], F32),
                             sb(f"{name}_b", [P, 1], F32), sb(f"{name}_r", [P, 4], F32))

        def wait(eng, semaphore, value):
            if isinstance(value, int) and value <= 0:
                return
            eng.wait_ge(semaphore, value)

        def plain(eng):
            eng.nop(nofuse=True)

        def rolled(eng, lo, hi, body):
            if lo == 0:
                body(0)
                lo = 1
            if hi - lo == 1:
                body(lo)
            elif hi > lo:
                with eng.Fori(lo, hi) as n:
                    body(n)

        x_rows = x.rearrange("(g p) c -> g p c", p=P)
        out_rows = out.rearrange("(g p) c -> g p c", p=P)
        o_rows = o_dram.rearrange("(g p) c -> g p c", p=P)
        o_heads = o_dram.rearrange("(b i p) (h d) -> b h p i d", b=B, p=P, d=D)

        block = ctx.enter_context(nc.Block())

        @block.sync
        def _(sp):
            sp.dma_start(w_f32[:], wqkv.rearrange("m (k p) n -> p m k n", p=P)).then_inc(weights_in, 16)
            sp.dma_start(tab_sb[:], table.rearrange("(o r) h -> o r h", o=1).to_broadcast([P, NBUCKET, H])
                         ).then_inc(table_in, 16)

            def load_head(g):
                wait(sp, xh_ready, g)
                sp.dma_start(xh[:], x_rows[g]).then_inc(xh_in, 16)

            def load_tail(g):
                if isinstance(g, int):
                    wait(sp, x2_ready, g)
                else:
                    sp.wait_ge(x2_ready, g)
                sp.dma_start(o_cur[:], o_rows[g]).then_inc(o_cur_in, 16)
                sp.dma_start(x_res[:], x_rows[g]).then_inc(x_res_in, 16)

            def store_out(g):
                sp.wait_ge(out_ready, g + 1)
                sp.dma_start(out_rows[g], out_sb[:]).then_inc(out_stored, 16)

            def spread_qk(h):
                rows = slice(D * h, D * h + D)
                sp.dma_start(q_pair[h][0:D, :], q_stage[rows, 0, :]).then_inc(qk_in[h], 16)
                sp.dma_start(q_pair[h][D:P, :], q_stage[rows, 1, :]).then_inc(qk_in[h], 16)
                sp.dma_start(k_twice[h][0:D, :, :], k_stage[rows, :, :]).then_inc(qk_in[h], 16)
                sp.dma_start(k_twice[h][D:P, :, :], k_stage[rows, :, :]).then_inc(qk_in[h], 16)

            def spread_v(h):
                sp.dma_start(v_head[h][:].rearrange("p i (a d) -> p i a d", a=2),
                             v_stage[:, :, h, :, :]).then_inc(v_in[h], 16)

            load_head(0)
            for dst, src in ((wp_sb, wp), (wr_sb, w_r), (wk_sb, w_k), (wv_sb, w_v)):
                sp.dma_start(dst[:], src.rearrange("(k p) n -> p k n", p=P)).then_inc(small_in, 16)
            sp.dma_start(bp_sb[:], bp.rearrange("(o c) -> o c", o=1).to_broadcast([P, C])).then_inc(small_in, 16)
            for m, mu in enumerate((mu_r, mu_k)):
                sp.dma_start(mu_sb[:, m, :], mu.rearrange("(k p) -> p k", p=P),
                             allow_slow_non_contiguous=True).then_inc(small_in, 16)
            rolled(sp, 1, HEAD_LEAD, load_head)

            sp.wait_ge(vec_setup, 7)
            sp.dma_start(band_dram.rearrange("h (p j) -> p h j", p=P), band_src[:]).then_inc(band_out, 16)
            sp.wait_ge(band_out, 16)
            shifted = band_dram[:, P - 1:P - 1 + P * (ROW - 1)].rearrange("h (p j) -> p h j", j=ROW - 1)
            sp.dma_start(band[:], shifted[:, :, 0:WIN]).then_inc(band_in, 16)

            sp.wait_ge(misc_free, HEAD_LEAD + len(NEXT_TASKS))
            for h in range(2):
                spread_qk(h)
                spread_v(h)

            for seg in segments:
                def body(n, seg=seg):
                    if seg.tail:
                        load_tail(n - TAIL_LAG)
                    if seg.head:
                        load_head(n + HEAD_LEAD)
                    for h in range(2):
                        if seg.next:
                            if h == 0:
                                sp.wait_ge(misc_free, seg.index(n, "k1") + 1)
                            sp.wait_ge(scored, UNITS * n + NB * (h + 1))
                            spread_qk(h)
                            if h == 0:
                                sp.wait_ge(misc_free, seg.index(n, "v1") + 1)
                            sp.wait_ge(pv_done, UNITS * n + NB * (h + 1))
                            spread_v(h)
                    if seg.tail:
                        store_out(n - TAIL_LAG)
                rolled(sp, seg.lo, seg.hi, body)

            def last_tails(g):
                load_tail(g)
                store_out(g)
            for h in range(2):
                sp.wait_ge(o_stored[h], 16 * N)
            rolled(sp, G - TAIL_LAG, G, last_tails)
            sp.wait_ge(out_stored, 16 * G)

        @block.tensor
        def _(pe):
            def misc_open(index):
                pe.wait_ge(misc_free, index) if not isinstance(index, int) or index > 0 else None

            def head_transpose(g, index):
                pe.wait_ge(xh_ready, g + 1)
                misc_open(index)
                for k in range(KT):
                    last = pe.transpose(misc[:, k * P:(k + 1) * P], xh_norm[:, k * P:(k + 1) * P], ident[:])
                last.then_inc(misc_full, 1)

            def project_qk(which, half, pair, ring, index):
                misc_open(index)
                step = 0
                for k in range(KT):
                    for w, a in ((0, 0), (1, 0), (0, 1)):
                        last = pe.matmul(misc[:], w_split[:, w, which, k, bass.ds(pair * P, P)],
                                         xT[:, a, k, bass.ds(ring * T + half * 512, 512)],
                                         start=step == 0, stop=step == 3 * KT - 1)
                        step += 1
                last.then_inc(misc_full, 1)

            def project_v(half, pair, ring, index):
                misc_open(index)
                for i in range(4):
                    step = 0
                    for k in range(KT):
                        for w, a in ((0, 0), (1, 0), (0, 1)):
                            last = pe.matmul(misc[:, i * P:(i + 1) * P],
                                             xT[:, a, k, bass.ds(ring * T + (half * 4 + i) * P, P)],
                                             w_split[:, w, 2, k, bass.ds(pair * P, P)],
                                             start=step == 0, stop=step == 3 * KT - 1)
                            step += 1
                last.then_inc(misc_full, 1)

            def next_task(name, n, index):
                pair, ring = pe.snap((n + 1) % NPAIR), pe.snap(((n + 1) // NPAIR) % 2)
                if name[0] == "v":
                    project_v(int(name[1]), pair, ring, index)
                else:
                    project_qk("qk".index(name[0]), int(name[1]), pair, ring, index)

            def tail_task(name, g, index):
                if name in ("ot0", "ot1"):
                    half = int(name[2])
                    if half == 0:
                        pe.wait_ge(o_cur_in, 16 * (g + 1))
                    misc_open(index)
                    for j in range(4):
                        c = half * 4 + j
                        last = pe.transpose(misc[:, j * P:(j + 1) * P], o_cur[:, c * P:(c + 1) * P], ident[:])
                elif name == "proj":
                    misc_open(index)
                    for c in range(H * D // P):
                        last = pe.matmul(misc[:, 0:C], oT[:, c, :], wp_sb[:, c, :], start=c == 0,
                                         stop=c == H * D // P - 1)
                elif name == "x2t":
                    pe.wait_ge(x2_normed, g + 1)
                    misc_open(index)
                    for k in range(KT):
                        last = pe.transpose(misc[:, k * P:(k + 1) * P], x2_norm[:, k * P:(k + 1) * P], ident[:])
                elif name == "rk":
                    pe.wait_ge(mixed_ready, 2 * KT * (g + 1))
                    misc_open(index)
                    for k in range(KT):
                        pe.matmul(misc[:, 0:C], mixed[:, 0, k, :], wr_sb[:, k, :], start=k == 0, stop=k == KT - 1)
                    for m in range(KT):
                        for k in range(KT):
                            last = pe.matmul(misc[:, C + m * P:C + (m + 1) * P], wk_sb[:, k, m * P:(m + 1) * P],
                                             mixed[:, 1, k, :], start=k == 0, stop=k == KT - 1)
                else:
                    pe.wait_ge(k_act_ready, g + 1)
                    misc_open(index)
                    for k in range(KT):
                        last = pe.matmul(misc[:, 0:C], k_act[:, k, :], wv_sb[:, k, :], start=k == 0,
                                         stop=k == KT - 1)
                last.then_inc(misc_full, 1)

            def score(n, u):
                h, i, unit = (u % UNITS) // NB, u % NB, UNITS * n + u
                if i == 0:
                    pe.wait_ge(qk_in[h], 64 * (n + 1 + u // UNITS))
                wait(pe, exp_done, unit - 1)
                for c in range((i + 4) // 4):
                    cols = min(512, (i + 1) * P - c * 512)
                    for a in range(2):
                        last = pe.matmul(scores[:, u % 2, c * 512:c * 512 + cols], q_pair[h][:, i * P:(i + 1) * P],
                                         k_twice[h][:, a, c * 512:c * 512 + cols], start=a == 0, stop=a == 1)
                last.then_inc(scored, 1)

            def transpose_probs(n, u):
                pe.wait_ge(exp_done, UNITS * n + u + 1)
                for c, blocks in chunks(u % NB):
                    k = CHUNK0[u] + c
                    wait(pe, lo_done, CHUNKS * n + k - 1)
                    for j in range(blocks):
                        s = 4 * c + j
                        last = pe.transpose(probsT_ps[k % 2][:, j, :], probs[:, u % 2, s * P:(s + 1) * P], ident[:])
                    last.then_inc(transposed, 1)

            def weigh_values(n, u):
                h, i = u // NB, u % NB
                if i == 0:
                    pe.wait_ge(v_in[h], 16 * (n + 1))
                pe.wait_ge(lo_done, CHUNKS * n + CHUNK0[u + 1])
                wait(pe, parts_ready, UNITS * n + u)
                for s in range(i + 1):
                    for a in range(2):
                        last = pe.matmul(o_ps[:, 0:2 * D], probsT[:, u % 2, a, s, :], v_head[h][:, s, :],
                                         start=s == 0 and a == 0, stop=s == i and a == 1)
                last.then_inc(pv_done, 1)

            pe.wait_ge(ident_ready, 1)
            rolled(pe, 0, HEAD_LEAD, lambda g: head_transpose(g, g))
            pe.wait_ge(split_lo, 3)
            for k, name in enumerate(NEXT_TASKS):
                if name[0] == "v":
                    project_v(int(name[1]), 0, 0, HEAD_LEAD + k)
                else:
                    project_qk("qk".index(name[0]), int(name[1]), 0, 0, HEAD_LEAD + k)
            score(0, 0)
            score(0, 1)
            pe.wait_ge(small_in, 16 * 7)
            pe.wait_ge(vec_setup, 8)
            for seg in segments:
                def body(n, seg=seg):
                    for u in range(UNITS):
                        transpose_probs(n, u)
                        if u + 2 < UNITS or seg.next:
                            score(n, u + 2)
                        name = seg.in_slot.get(u)
                        if name in NEXT_TASKS:
                            next_task(name, n, seg.index(n, name))
                        elif name in TAIL_TASKS:
                            tail_task(name, n - TAIL_LAG, seg.index(n, name))
                        elif name in HEAD_TASKS:
                            head_transpose(n + HEAD_LEAD, seg.index(n, name))
                        weigh_values(n, u)
                rolled(pe, seg.lo, seg.hi, body)

            def last_tails(g):
                for k, name in enumerate(TAIL_TASKS):
                    tail_task(name, g, tail_base + len(TAIL_TASKS) * (g - (G - TAIL_LAG)) + k)
            rolled(pe, G - TAIL_LAG, G, last_tails)

        @block.scalar
        def _(act):
            def evacuate_high(dst, src, index):
                act.wait_ge(misc_full, index + 1)
                nc.scalar.copy(dst, src).then_inc(misc_hi, 1)

            def head_high(g, index):
                at = act.snap(g % (RING // P) * P) if not isinstance(g, int) else g % (RING // P) * P
                evacuate_high(xT[:, 0, :, bass.ds(at, P)], misc[:, 0:C].rearrange("p (k t) -> p k t", k=KT), index)

            def next_high(name, pairs_before, index):
                half = int(name[1])
                if name == "q0":
                    wait(act, qk_in[1], 64 * pairs_before)
                if name == "v0":
                    wait(act, v_in[1], 16 * pairs_before)
                if name[0] == "v":
                    evacuate_high(v_stage[:, 4 * half:4 * half + 4, :, 0, :],
                                  misc[:].rearrange("p (i h d) -> p i h d", i=4, h=2), index)
                else:
                    stage = q_stage if name[0] == "q" else k_stage
                    evacuate_high(stage[:, 0, half * 512:(half + 1) * 512], misc[:], index)

            def tail_step(name, g, index):
                if name in ("ot0", "ot1"):
                    half = int(name[2])
                    act.wait_ge(misc_full, index + 1)
                    nc.scalar.copy(oT[:, half * 4:half * 4 + 4, :],
                                   misc[:].rearrange("p (c t) -> p c t", c=4)).then_inc(misc_free, 1)
                elif name == "x2t":
                    act.wait_ge(misc_full, index + 1)
                    act.wait_ge(carried, KT * (g + 1))
                    nc.scalar.copy(x2T[:, :, 1:P + 1],
                                   misc[:, 0:C].rearrange("p (k t) -> p k t", k=KT)).then_inc(misc_free, 1)
                elif name == "rk":
                    act.wait_ge(misc_full, index + 1)
                    nc.scalar.activation(gate_exp[:], misc[:, 0:C], ACT.Exp, scale=-1.0).then_inc(gate_exped, 1)
                    nc.scalar.activation(k_relu[:], misc[:, C:2 * C].rearrange("p (k t) -> p k t", k=KT),
                                         ACT.Relu).then_inc(misc_free, 1)

            def exponential(n, u):
                unit, i = UNITS * n + u, u % NB
                act.wait_ge(bias_ready, unit + 1)
                wait(act, transposed, CHUNKS * n + chunks_before(u - 1))
                wait(act, inv_ready, unit - 3)
                cols = (i + 1) * P
                nc.scalar.activation(probs[:, u % 2, 0:cols], scores[:, u % 2, 0:cols], ACT.Exp,
                                     bias=exp_bias[:, u % 4:u % 4 + 1], scale=score_unit[:],
                                     accum_out=row_sum[:, u % 4:u % 4 + 1]).then_inc(exp_done, 1)

            def high_parts(n, u):
                for c, blocks in chunks(u % NB):
                    k = CHUNKS * n + CHUNK0[u] + c
                    act.wait_ge(transposed, k + 1)
                    if c == 0:
                        wait(act, pv_done, UNITS * n + u - 1)
                    nc.scalar.copy(probsT[:, u % 2, 0, 4 * c:4 * c + blocks, :],
                                   probsT_ps[(CHUNK0[u] + c) % 2][:, 0:blocks, :]).then_inc(hi_done, 1)

            def scale_output(n, u):
                unit = UNITS * n + u
                act.wait_ge(pv_done, unit + 1)
                act.wait_ge(inv_ready, unit + 1)
                wait(act, o_added, unit - 1)
                nc.scalar.activation(o_parts[:, u % 2, :], o_ps[:, 0:2 * D], ACT.Copy,
                                     scale=inv_sum[:, u % 4:u % 4 + 1]).then_inc(parts_ready, 1)

            rolled(act, 0, HEAD_LEAD, lambda g: head_high(g, g))
            for k, name in enumerate(NEXT_TASKS):
                next_high(name, 0, HEAD_LEAD + k)
            exponential(0, 0)
            exponential(0, 1)
            for seg in segments:
                def body(n, seg=seg):
                    for u in range(UNITS):
                        high_parts(n, u)
                        if u > 0:
                            scale_output(n, u - 1)
                        elif not isinstance(n, int) or n > 0:
                            scale_output(n, -1)
                        name = seg.in_slot.get(u)
                        if name in NEXT_TASKS:
                            next_high(name, n + 1, seg.index(n, name))
                        elif name in TAIL_TASKS:
                            tail_step(name, n - TAIL_LAG, seg.index(n, name))
                        elif name in HEAD_TASKS:
                            head_high(n + HEAD_LEAD, seg.index(n, name))
                        if u + 2 < UNITS or seg.next:
                            exponential(n, u + 2)
                rolled(act, seg.lo, seg.hi, body)
            scale_output(N - 1, UNITS - 1)

            def last_tails(g):
                for k, name in enumerate(TAIL_TASKS):
                    tail_step(name, g, tail_base + len(TAIL_TASKS) * (g - (G - TAIL_LAG)) + k)
            rolled(act, G - TAIL_LAG, G, last_tails)

        @block.vector
        def _(dve):
            def statistics(name, src, g, stats_sem, aggr_sem, ready_sem, ready, used_sem):
                bn, mv = ln_bufs[name][:2]
                wait(dve, ready_sem, ready)
                dve.bn_stats(bn[:], src).then_inc(stats_sem, 1)
                dve.wait_ge(stats_sem, g + 1)
                wait(dve, used_sem, g)
                plain(dve)
                dve.bn_aggr(mv[:], bn[:]).then_inc(aggr_sem, 1)

            def evacuate_low(dst, src, high, hi_count):
                dve.wait_ge(misc_hi, hi_count)
                dve.tensor_tensor(dst, src, high, ALU.subtract).then_inc(misc_free, 1)

            def head_low(g, hi_count):
                at = dve.snap(g % (RING // P) * P) if not isinstance(g, int) else g % (RING // P) * P
                evacuate_low(xT[:, 1, :, bass.ds(at, P)], misc[:, 0:C].rearrange("p (k t) -> p k t", k=KT),
                             xT[:, 0, :, bass.ds(at, P)], hi_count)

            def next_low(name, hi_count):
                half = int(name[1])
                if name[0] == "v":
                    evacuate_low(v_stage[:, 4 * half:4 * half + 4, :, 1, :],
                                 misc[:].rearrange("p (i h d) -> p i h d", i=4, h=2),
                                 v_stage[:, 4 * half:4 * half + 4, :, 0, :], hi_count)
                else:
                    stage = q_stage if name[0] == "q" else k_stage
                    cols = slice(half * 512, (half + 1) * 512)
                    evacuate_low(stage[:, 1, cols], misc[:], stage[:, 0, cols], hi_count)

            def tail_step(name, g, index):
                if name == "proj":
                    dve.wait_ge(misc_full, index + 1)
                    wait(dve, y_normed, g)
                    dve.tensor_tensor(y[:], misc[:, 0:C], bp_sb[:], ALU.add).then_inc(misc_free, 1)
                    statistics("y", y[:], g, y_stats, y_aggr, misc_free, index + 1, y_normed)
                elif name == "x2stats":
                    statistics("x2", x2[:], g, x2_stats, x2_aggr, x2_ready, g + 1, x2_normed)
                elif name == "mix":
                    dve.wait_ge(delta_ready, g + 1)
                    for m in range(2):
                        for k in range(KT):
                            dve.scalar_tensor_tensor(mixed[:, m, k, :], delta[:, k, :], mu_sb[:, m, k:k + 1],
                                                     x2T[:, k, 0:P], ALU.mult, ALU.add).then_inc(mixed_ready, 1)
                elif name == "gate":
                    dve.wait_ge(den_ready, g + 1)
                    dve.reciprocal(gate[:], gate_den[:]).then_inc(gate_ready, 1)
                elif name == "ffn":
                    dve.wait_ge(misc_full, index + 1)
                    dve.wait_ge(gate_ready, g + 1)
                    wait(dve, z_normed, g)
                    dve.tensor_tensor(z[:], misc[:, 0:C], gate[:], ALU.mult).then_inc(misc_free, 1)
                    statistics("z", z[:], g, z_stats, z_aggr, misc_free, index + 1, z_normed)

            def row_bias(n, u, pair):
                h, i, unit = (u % UNITS) // NB, u % NB, UNITS * n + u
                lo = i * P - MAX_REL if i else 0
                hi = (i + 1) * P
                win = scores[:, u % 2, lo:hi]
                dve.wait_ge(scored, unit + 1)
                dve.tensor_tensor(win, win, band[:, bass.ds(2 * pair + h, 1), WIN - (hi - lo):WIN].rearrange(
                    "p o j -> p (o j)"), ALU.add).then_inc(band_added, 1)
                dve.wait_ge(band_added, unit + 1)
                dve.tensor_reduce(neg_max[:, u % 4:u % 4 + 1], scores[:, u % 2, 0:hi], AX.X, ALU.max,
                                  negate=True).then_inc(max_ready, 1)
                dve.wait_ge(max_ready, unit + 1)
                wait(dve, exp_done, unit - 3)
                dve.tensor_scalar(exp_bias[:, u % 4:u % 4 + 1], neg_max[:, u % 4:u % 4 + 1], score_unit[:, 0:1],
                                  P_SHIFT, ALU.mult, ALU.add).then_inc(bias_ready, 1)

            def low_parts(n, u):
                for c, blocks in chunks(u % NB):
                    k = CHUNKS * n + CHUNK0[u] + c
                    dve.wait_ge(hi_done, k + 1)
                    dve.tensor_tensor(probsT[:, u % 2, 1, 4 * c:4 * c + blocks, :],
                                      probsT_ps[(CHUNK0[u] + c) % 2][:, 0:blocks, :],
                                      probsT[:, u % 2, 0, 4 * c:4 * c + blocks, :], ALU.subtract).then_inc(lo_done, 1)

            def invert_sum(n, u):
                unit = UNITS * n + u
                dve.wait_ge(exp_done, unit + 1)
                wait(dve, parts_ready, unit - 3)
                dve.reciprocal(inv_sum[:, u % 4:u % 4 + 1], row_sum[:, u % 4:u % 4 + 1]).then_inc(inv_ready, 1)

            def head_stats(g):
                statistics("xh", xh[:], g, xh_stats, xh_aggr, xh_in, 16 * (g + 1), xh_ready)

            dve.wait_ge(weights_in, 16)
            for m in range(3):
                last = dve.tensor_reduce(top[:, m:m + 1], w_f32[:, m, :, :], AX.XY, ALU.max,
                                         apply_absolute_value=True)
            last.then_inc(top_ready, 1)
            dve.wait_ge(top_reduced, 1)
            dve.tensor_scalar(top_all[:], top_all[:], 2.0 ** -40, None, ALU.max).then_inc(vec_setup, 1)
            dve.wait_ge(vec_setup, 1)
            dve.tensor_scalar(pow2[:].bitcast(I32), top_all[:].bitcast(I32), 0x7F800000, None,
                              ALU.bitwise_and).then_inc(vec_setup, 1)
            dve.wait_ge(vec_setup, 2)
            dve.reciprocal(inv2[:], pow2[:]).then_inc(vec_setup, 1)
            dve.wait_ge(vec_setup, 3)
            dve.tensor_scalar(w_scale[:], inv2[:], W_TOP, None, ALU.mult)
            dve.tensor_scalar(score_unit[:], pow2[:, 0:1], pow2[:, 1:2], D ** -0.5 / W_TOP ** 2, ALU.mult, ALU.mult)
            dve.tensor_scalar(band_unit[:], inv2[:, 0:1], inv2[:, 1:2], D ** 0.5 * W_TOP ** 2,
                              ALU.mult, ALU.mult).then_inc(vec_setup, 1)
            dve.wait_ge(vec_setup, 4)
            for m in range(3):
                dve.tensor_scalar(w_split[:, 0, m], w_f32[:, m], w_scale[:, m:m + 1], None,
                                  ALU.mult).then_inc(split_hi, 1)
            for m in range(3):
                dve.wait_ge(split_hi, m + 1)
                dve.scalar_tensor_tensor(w_split[:, 1, m], w_f32[:, m], w_scale[:, m:m + 1], w_split[:, 0, m],
                                         ALU.mult, ALU.subtract).then_inc(split_lo, 1)
            dve.wait_ge(table_in, 16)
            dve.memset(band_src[:, :, 0:P], 0.0)
            dve.memset(band_src[:, :, WIN:ROW], MASKED).then_inc(vec_setup, 1)
            dve.tensor_tensor(band_src[:, :, P:WIN], tab_sb[:, 1:1 + MAX_REL, :].rearrange("p r h -> p h r"),
                              tab_sb[:, 0:1, :].rearrange("p r h -> p h r").to_broadcast([P, H, MAX_REL]),
                              ALU.subtract).then_inc(vec_setup, 1)
            dve.wait_ge(vec_setup, 6)
            dve.tensor_scalar(band_src[:, :, P:WIN], band_src[:, :, P:WIN], band_unit[:, 0:1], None,
                              ALU.mult).then_inc(vec_setup, 1)
            dve.wait_ge(small_in, 16 * 7)
            dve.tensor_scalar(wp_sb[:], wp_sb[:], pow2[:, 2:3], 1.0 / W_TOP, ALU.mult, ALU.mult).then_inc(vec_setup, 1)

            def prologue_head(g):
                head_stats(g)
                head_low(g, g + 1)
            rolled(dve, 0, HEAD_LEAD, prologue_head)
            for k, name in enumerate(NEXT_TASKS):
                next_low(name, HEAD_LEAD + k + 1)
            dve.wait_ge(band_in, 16)
            row_bias(0, 0, 0)
            row_bias(0, 1, 0)

            two_part = {**NEXT_TASKS, **HEAD_TASKS}
            hi_base = HEAD_LEAD + len(NEXT_TASKS)
            for seg in segments:
                split = [name for name in seg.order if name in two_part]

                def body(n, seg=seg, split=split, hi_base=hi_base):
                    pair = n % NPAIR if isinstance(n, int) else dve.snap(n % NPAIR)
                    pair1 = (n + 1) % NPAIR if isinstance(n, int) else dve.snap((n + 1) % NPAIR)
                    for u in range(UNITS):
                        invert_sum(n, u)
                        low_parts(n, u)
                        if u + 2 < UNITS or seg.next:
                            row_bias(n, u + 2, pair if u + 2 < UNITS else pair1)
                        name = seg.in_slot.get(u)
                        if name in split:
                            count = hi_base + len(split) * (n - seg.lo) + split.index(name) + 1
                            if name in NEXT_TASKS:
                                next_low(name, count)
                            else:
                                head_low(n + HEAD_LEAD, count)
                        elif name in ("proj", "ffn"):
                            tail_step(name, n - TAIL_LAG, seg.index(n, name))
                        if seg.head and u == 9:
                            head_stats(n + HEAD_LEAD)
                        if seg.tail and u in (8, 12, 14):
                            tail_step({8: "x2stats", 12: "mix", 14: "gate"}[u], n - TAIL_LAG, None)
                rolled(dve, seg.lo, seg.hi, body)
                hi_base += len(split) * (seg.hi - seg.lo)

            def last_tails(g):
                first = tail_base + len(TAIL_TASKS) * (g - (G - TAIL_LAG))
                tail_step("proj", g, first + 2)
                tail_step("x2stats", g, None)
                tail_step("mix", g, None)
                tail_step("gate", g, None)
                tail_step("ffn", g, first + 5)
            rolled(dve, G - TAIL_LAG, G, last_tails)

        @block.gpsimd
        def _(pool):
            def normalise(name, dst, src, g, aggr_sem, pool_sem, done_sem, dst_free):
                _, mv, var, a, b, r = ln_bufs[name]
                count = LN_OPS * g
                wait(pool, done_sem, g)
                pool.wait_ge(aggr_sem, g + 1)
                plain(pool)
                pool.tensor_scalar(var[:], mv[:, 1:2], EPS, None, ALU.add).then_inc(pool_sem, 1)
                pool.wait_ge(pool_sem, count + 1)
                plain(pool)
                pool.tensor_scalar(r[:, 0:1].bitcast(I32), var[:].bitcast(I32), -0.5, RSQRT_SEED,
                                   ALU.mult, ALU.add).then_inc(pool_sem, 1)
                for k in range(NEWTON):
                    pool.wait_ge(pool_sem, count + 3 * k + 2)
                    plain(pool)
                    pool.tensor_scalar(a[:], r[:, k:k + 1], r[:, k:k + 1], var[:], ALU.mult,
                                       ALU.mult).then_inc(pool_sem, 1)
                    pool.wait_ge(pool_sem, count + 3 * k + 3)
                    plain(pool)
                    pool.tensor_scalar(b[:], a[:], -0.5, 1.5, ALU.mult, ALU.add).then_inc(pool_sem, 1)
                    pool.wait_ge(pool_sem, count + 3 * k + 4)
                    pool.tensor_tensor(r[:, k + 1:k + 2], r[:, k:k + 1], b[:], ALU.mult).then_inc(pool_sem, 1)
                pool.wait_ge(pool_sem, count + LN_OPS)
                wait(pool, *dst_free)
                plain(pool)
                pool.tensor_scalar(dst, src, mv[:, 0:1], r[:, NEWTON:NEWTON + 1], ALU.subtract,
                                   ALU.mult).then_inc(done_sem, 1)

            def add_parts(n, u):
                unit, h, i = UNITS * n + u, (u % UNITS) // NB, u % NB
                pool.wait_ge(parts_ready, unit + 1)
                if i == 0:
                    wait(pool, o_stored[h], 16 * n if u >= 0 else 16 * (n - 1))
                pool.tensor_tensor(o_stage[h][:, i, :], o_parts[:, u % 2, 0:D], o_parts[:, u % 2, D:2 * D],
                                   ALU.add).then_inc(o_added, 1)

            def store_head(n, h, b, pair):
                pool.wait_ge(o_added, UNITS * n + NB * (h + 1))
                pool.dma_start(o_heads[b, pair * 2 + h], o_stage[h][:]).then_inc(o_stored[h], 16)

            def tail_step(name, g):
                if name == "x2":
                    normalise("y", y_norm[:], y[:], g, y_aggr, y_pool, y_normed, (x2_ready, g))
                    pool.wait_ge(y_normed, g + 1)
                    pool.wait_ge(x_res_in, 16 * (g + 1))
                    wait(pool, out_ready, g)
                    pool.tensor_tensor(x2[:], x_res[:], y_norm[:], ALU.add).then_inc(x2_ready, 1)
                elif name == "x2_norm":
                    normalise("x2", x2_norm[:], x2[:], g, x2_aggr, x2_pool, x2_normed, (mixed_ready, 2 * KT * g))
                    for k in range(KT):
                        pool.tensor_tensor(x2T[:, k, 0:1], x2T[:, k, P:P + 1], keep_carry[:, bass.ds(g, 1)],
                                           ALU.mult).then_inc(carried, 1)
                elif name == "delta":
                    pool.tensor_tensor(delta[:], x2T[:, :, 1:P + 1], x2T[:, :, 0:P],
                                       ALU.subtract).then_inc(delta_ready, 1)
                elif name == "act":
                    pool.wait_ge(gate_exped, g + 1)
                    wait(pool, gate_ready, g)
                    plain(pool)
                    pool.tensor_scalar(gate_den[:], gate_exp[:], 1.0, None, ALU.add).then_inc(den_ready, 1)
                    pool.tensor_tensor(k_act[:], k_relu[:], k_relu[:], ALU.mult).then_inc(k_act_ready, 1)
                else:
                    normalise("z", z_norm[:], z[:], g, z_aggr, z_pool, z_normed, (out_ready, g))
                    pool.wait_ge(z_normed, g + 1)
                    wait(pool, out_stored, 16 * g)
                    pool.tensor_tensor(out_sb[:], x2[:], z_norm[:], ALU.add).then_inc(out_ready, 1)

            pool.memset(ident[:], 0.0).then_inc(pool_setup, 1)
            pool.wait_ge(pool_setup, 1)
            pool.affine_select(out=ident[:], in_=ident[:], compare_op=ALU.not_equal, fill=1.0, base=0,
                               pattern=[[-1, P]], channel_multiplier=1).then_inc(ident_ready, 1)
            pool.memset(keep_carry[:], 1.0).then_inc(pool_setup, 1)
            pool.memset(x2T[:], 0.0).then_inc(pool_setup, 1)
            pool.wait_ge(pool_setup, 3)
            pool.memset(keep_carry[:].rearrange("p (b i) -> p b i", i=NB)[:, :, 0:1], 0.0).then_inc(pool_setup, 1)
            pool.wait_ge(top_ready, 1)
            pool.partition_all_reduce(top_all[:], top[:], P, bass.bass_isa.ReduceOp.max).then_inc(top_reduced, 1)
            pool.wait_ge(pool_setup, 4)

            rolled(pool, 0, HEAD_LEAD, lambda g: normalise("xh", xh_norm[:], xh[:], g, xh_aggr, xh_pool, xh_ready,
                                                           (misc_free, g)))
            for seg in segments:
                def body(n, seg=seg):
                    g = n - TAIL_LAG
                    b, pair = (n // NPAIR, n % NPAIR) if isinstance(n, int) else (pool.snap(n // NPAIR),
                                                                                pool.snap(n % NPAIR))
                    for u in range(UNITS):
                        if u > 0:
                            add_parts(n, u - 1)
                        elif not isinstance(n, int) or n > 0:
                            add_parts(n, -1)
                            if isinstance(n, int):
                                store_head(n - 1, 1, (n - 1) // NPAIR, (n - 1) % NPAIR)
                            else:
                                store_head(n - 1, 1, pool.snap((n - 1) // NPAIR), pool.snap((n - 1) % NPAIR))
                        if u == NB:
                            store_head(n, 0, b, pair)
                        if seg.head and u == 10:
                            normalise("xh", xh_norm[:], xh[:], n + HEAD_LEAD, xh_aggr, xh_pool, xh_ready,
                                      (misc_free, seg.index(n, "q0")))
                        if seg.tail and u == 7:
                            tail_step("x2", g)
                        if seg.tail and u == 9:
                            tail_step("x2_norm", g)
                        if seg.tail and u == 12:
                            pool.wait_ge(misc_free, seg.index(n, "x2t") + 1)
                            tail_step("delta", g)
                        if seg.tail and u == 14:
                            pool.wait_ge(misc_free, seg.index(n, "rk") + 1)
                            tail_step("act", g)
                    if seg.tail:
                        tail_step("out", g)
                rolled(pool, seg.lo, seg.hi, body)
            add_parts(N - 1, UNITS - 1)
            store_head(N - 1, 1, B - 1, NPAIR - 1)

            def last_tails(g):
                first = tail_base + len(TAIL_TASKS) * (g - (G - TAIL_LAG))
                tail_step("x2", g)
                tail_step("x2_norm", g)
                pool.wait_ge(misc_free, first + 4)
                tail_step("delta", g)
                pool.wait_ge(misc_free, first + 5)
                tail_step("act", g)
                tail_step("out", g)
            rolled(pool, G - TAIL_LAG, G, last_tails)


def kernel(**inputs):
    import numpy as np
    import concourse.bacc as bacc
    from concourse.bass_utils import run_bass_kernel_spmd

    a = {k.split("_", 1)[1]: np.asarray(v) for k, v in inputs.items()}
    heads_last = [a[f"attn_{w}"].transpose(1, 0, 2).reshape(C, H * D) for w in ("Wq", "Wk", "Wv")]
    arrays = {
        "x": a["attn_x"].reshape(B * T, C),
        "wqkv": np.stack(heads_last),
        "wp": a["attn_Wp"],
        "bp": a["attn_bp"],
        "table": a["attn_rel_table"],
        "w_r": a["ffn_W_r"].T,
        "w_k": a["ffn_W_k"].T,
        "w_v": a["ffn_W_v"].T,
        "mu_r": a["ffn_mu_r"],
        "mu_k": a["ffn_mu_k"],
    }
    arrays = {k: np.ascontiguousarray(v) for k, v in arrays.items()}
    nc = bacc.Bacc("TRN2", target_bir_lowering=False, num_devices=1)
    args = [nc.dram_tensor(k, v.shape, mybir.dt.from_np(v.dtype), kind="ExternalInput").ap()
            for k, v in arrays.items()]
    out = nc.dram_tensor("out", [B * T, C], F32, kind="ExternalOutput").ap()
    build(nc, *args, out)
    r = run_bass_kernel_spmd(nc, [arrays], core_ids=[0])
    return r.results[0]["out"].reshape(B, T, C)
```

```python
from contextlib import ExitStack
from math import log

import concourse.bass as bass
from concourse import mybir

P = 128
B, T, C, H, D = 8, 1024, 256, 16, 64
NBUCKET, MAX_REL = 33, 16
KT = C // P
NB = T // P
NPAIR = H // 2
N = B * NPAIR
G = B * NB
UNITS = 2 * NB
HEAD_LEAD, TAIL_LAG = NB + 1, NPAIR + 1
RING = 2 * T
WIN = P + MAX_REL
ROW = WIN + P
MASKED = -3.0e38
EPS = 1e-5
W_TOP = 64.0
P_SHIFT = 14 * log(2.0)
RSQRT_SEED = float(0x5F3759DF)
NEWTON = 3
LN_OPS = 2 + 3 * NEWTON

ALU = mybir.AluOpType
ACT = mybir.ActivationFunctionType
AX = mybir.AxisListType
F32, F16, I32 = mybir.dt.float32, mybir.dt.float16, mybir.dt.int32

NEXT_TASKS = {"q0": 0, "q1": 1, "k0": 3, "k1": 4, "v0": 7, "v1": 11}
FRONT_TASKS = {"ot0": 6, "ot1": 8, "proj": 10}
BACK_TASKS = {"x2t": 2, "rk": 5, "ffn": 9}
HEAD_TASKS = {"xt": 12}
LAST_ORDER = ["ot0", "x2t", "ot1", "proj", "rk", "ffn"]
VEC_STEPS = {3: "mix", 4: "head", 8: "gate", 13: "x2stats"}
POOL_STEPS = {3: "delta", 5: "head", 6: "act", 10: "out", 12: "x2", 14: "x2_norm"}
BACK_STEPS = ("mix", "gate", "delta", "act", "out")
ORDER = [0, 7, 1, 6, 2, 5, 3, 4]


class Segment:

    def __init__(self, lo, hi, base):
        self.lo, self.hi, self.base = lo, hi, base
        self.next = lo < N - 1
        self.head = lo < G - HEAD_LEAD
        self.front = lo >= TAIL_LAG
        self.back = lo >= TAIL_LAG + 1
        slots = {**(NEXT_TASKS if self.next else {}), **(FRONT_TASKS if self.front else {}),
                 **(BACK_TASKS if self.back else {}), **(HEAD_TASKS if self.head else {})}
        self.order = sorted(slots, key=slots.get)
        self.in_slot = {slots[name]: name for name in self.order}
        self.end_base = base + len(self.order) * (hi - lo)

    def tail_block(self, n, name):
        return n - TAIL_LAG - (name in BACK_TASKS or name in BACK_STEPS)

    def has(self, name):
        return self.head if name == "head" else self.back if name in BACK_STEPS else self.front

    def index(self, n, name):
        return self.base + len(self.order) * (n - self.lo) + self.order.index(name)


def plan():
    segments, base = [], HEAD_LEAD + len(NEXT_TASKS)
    for lo, hi in ((0, 1), (1, TAIL_LAG), (TAIL_LAG, TAIL_LAG + 1),
                   (TAIL_LAG + 1, TAIL_LAG + 2), (TAIL_LAG + 2, G - HEAD_LEAD), (G - HEAD_LEAD, N - 1), (N - 1, N)):
        segments.append(Segment(lo, hi, base))
        base = segments[-1].end_base
    return segments, base


def chunks(i):
    return [(c, min(4, i + 1 - 4 * c)) for c in range((i + 4) // 4)]


def head_block(u):
    return u % UNITS // NB, ORDER[u % NB]


CHUNK0 = [sum(len(chunks(head_block(k)[1])) for k in range(u)) for u in range(UNITS + 1)]
CHUNKS = CHUNK0[UNITS]


def chunks_before(u):
    return CHUNKS * (u // UNITS) + CHUNK0[u % UNITS]


def build(nc, x, wqkv, wp, bp, table, w_r, w_k, w_v, mu_r, mu_k, out):
    segments, tail_base = plan()
    with ExitStack() as ctx:
        def sb(name, shape, dt):
            return ctx.enter_context(nc.sbuf_tensor(name, shape, dt))

        def ps(name, shape):
            return ctx.enter_context(nc.psum_tensor(name, shape, F32))

        def sem(name):
            return ctx.enter_context(nc.semaphore(name))

        o_dram = nc.dram_tensor("o_scratch", [B * T, H * D], F32, kind="Internal").ap()
        band_dram = nc.dram_tensor("band_scratch", [H, P * ROW], F32, kind="Internal").ap()

        ident = sb("ident", [P, P], F32)
        w_f32 = sb("w_f32", [P, 3, KT, H * D], F32)
        w_split = sb("w_split", [P, 2, 3, KT, H * D], F16)
        wp_sb = sb("wp_sb", [P, H * D // P, C], F32)
        wr_sb = sb("wr_sb", [P, KT, C], F32)
        wk_sb = sb("wk_sb", [P, KT, C], F32)
        wv_sb = sb("wv_sb", [P, KT, C], F32)
        bp_sb = sb("bp_sb", [P, C], F32)
        mu_sb = sb("mu_sb", [P, 2, KT], F32)
        tab_sb = sb("tab_sb", [P, NBUCKET, H], F32)
        band_src = sb("band_src", [P, H, ROW], F32)
        band = sb("band", [P, H, WIN], F32)
        top = sb("top", [P, 3], F32)
        top_all = sb("top_all", [P, 3], F32)
        pow2 = sb("pow2", [P, 3], F32)
        inv2 = sb("inv2", [P, 3], F32)
        w_scale = sb("w_scale", [P, 3], F32)
        score_unit = sb("score_unit", [P, 1], F32)
        neg_unit = sb("neg_unit", [P, 1], F32)
        band_unit = sb("band_unit", [P, 1], F32)
        keep_carry = sb("keep_carry", [P, G], F32)

        xh = sb("xh", [P, C], F32)
        xh_norm = sb("xh_norm", [P, C], F32)
        xT = sb("xT", [P, 2, KT, RING], F16)

        q_stage = sb("q_stage", [P, 2, T], F16)
        k_stage = sb("k_stage", [P, 2, T], F16)
        v_stage = sb("v_stage", [P, NB, 2, 2, D], F16)
        q_pair = [sb(f"q_pair{h}", [P, T], F16) for h in range(2)]
        k_twice = [sb(f"k_twice{h}", [P, 2, T], F16) for h in range(2)]
        v_head = [sb(f"v_head{h}", [P, NB, 2 * D], F16) for h in range(2)]

        probs = sb("probs", [P, 2, T], F32)
        probsT = sb("probsT", [P, 2, 2, NB, P], F16)
        row_max = sb("row_max", [P, 4], F32)
        bias_row = [sb(f"bias_row{h}", [P, T], F32) for h in range(2)]
        exp_bias = sb("exp_bias", [P, 4], F32)
        row_sum = sb("row_sum", [P, 4], F32)
        inv_sum = sb("inv_sum", [P, 4], F32)
        o_parts = sb("o_parts", [P, 4, 2 * D], F32)
        o_stage = [sb(f"o_stage{h}", [P, NB, D], F32) for h in range(2)]

        o_cur = sb("o_cur", [P, H * D], F32)
        oT = sb("oT", [P, H * D // P, P], F32)
        x_res = sb("x_res", [P, C], F32)
        y = sb("y", [P, C], F32)
        y_norm = sb("y_norm", [P, C], F32)
        x2 = sb("x2", [P, C], F32)
        x2_keep = sb("x2_keep", [P, C], F32)
        x2_norm = sb("x2_norm", [P, C], F32)
        x2T = sb("x2T", [P, KT, P + 1], F32)
        delta = sb("delta", [P, KT, P], F32)
        mixed = sb("mixed", [P, 2, KT, P], F32)
        gate_exp = sb("gate_exp", [P, C], F32)
        gate_den = sb("gate_den", [P, C], F32)
        gate = sb("gate", [P, C], F32)
        k_relu = sb("k_relu", [P, KT, P], F32)
        k_act = sb("k_act", [P, KT, P], F32)
        z = sb("z", [P, C], F32)
        z_norm = sb("z_norm", [P, C], F32)
        out_sb = sb("out_sb", [P, C], F32)

        scores = ps("scores", [P, 2, T])
        probsT_ps = [ps(f"probsT_ps{k}", [P, 4, P]) for k in range(2)]
        o_ps = ps("o_ps", [P, 512])
        misc = ps("misc", [P, 512])

        weights_in, small_in = sem("weights_in"), sem("small_in")
        table_in, band_out, band_in = sem("table_in"), sem("band_out"), sem("band_in")
        pool_setup, top_ready, top_reduced = sem("pool_setup"), sem("top_ready"), sem("top_reduced")
        vec_setup, split_hi, split_lo = sem("vec_setup"), sem("split_hi"), sem("split_lo")
        ident_ready = sem("ident_ready")
        misc_full, misc_free, misc_hi = sem("misc_full"), sem("misc_free"), sem("misc_hi")
        xh_in, xh_stats, xh_aggr = sem("xh_in"), sem("xh_stats"), sem("xh_aggr")
        xh_pool, xh_ready = sem("xh_pool"), sem("xh_ready")
        qk_in = [sem(f"qk_in{h}") for h in range(2)]
        v_in = [sem(f"v_in{h}") for h in range(2)]
        o_stored = [sem(f"o_stored{h}") for h in range(2)]
        scored, max_ready = sem("scored"), sem("max_ready")
        bias_row_in = [sem(f"bias_row_in{h}") for h in range(2)]
        bias_ready, exp_done, transposed = sem("bias_ready"), sem("exp_done"), sem("transposed")
        hi_done, lo_done, pv_done = sem("hi_done"), sem("lo_done"), sem("pv_done")
        inv_ready, parts_ready, o_added = sem("inv_ready"), sem("parts_ready"), sem("o_added")
        o_cur_in, x_res_in = sem("o_cur_in"), sem("x_res_in")
        y_ready, y_stats, y_aggr, y_pool, y_normed = (
            sem("y_ready"), sem("y_stats"), sem("y_aggr"), sem("y_pool"), sem("y_normed"))
        x2_ready, x2_stats, x2_aggr, x2_pool, x2_normed = (
            sem("x2_ready"), sem("x2_stats"), sem("x2_aggr"), sem("x2_pool"), sem("x2_normed"))
        carried, delta_ready, mixed_ready = sem("carried"), sem("delta_ready"), sem("mixed_ready")
        gate_exped, relued, den_ready, gate_ready, k_act_ready = (
            sem("gate_exped"), sem("relued"), sem("den_ready"), sem("gate_ready"), sem("k_act_ready"))
        z_ready, z_stats, z_aggr, z_pool, z_normed = (
            sem("z_ready"), sem("z_stats"), sem("z_aggr"), sem("z_pool"), sem("z_normed"))
        out_ready, out_stored, x2_kept = sem("out_ready"), sem("out_stored"), sem("x2_kept")

        ln_bufs = {}
        for name in ("xh", "y", "x2", "z"):
            ln_bufs[name] = (sb(f"{name}_bn", [P, 6], F32), sb(f"{name}_mv", [P, 2], F32),
                             sb(f"{name}_var", [P, 1], F32), sb(f"{name}_a", [P, 1], F32),
                             sb(f"{name}_b", [P, 1], F32), sb(f"{name}_r", [P, 4], F32))

        def wait(eng, semaphore, value):
            if isinstance(value, int) and value <= 0:
                return
            eng.wait_ge(semaphore, value)

        def last_index(g, name):
            order = LAST_ORDER if not isinstance(g, int) or g < G else list(BACK_TASKS)
            return tail_base + len(LAST_ORDER) * (g - (G - TAIL_LAG)) + order.index(name)

        def plain(eng):
            eng.nop(nofuse=True)

        def rolled(eng, lo, hi, body):
            if lo == 0:
                body(0)
                lo = 1
            if hi - lo == 1:
                body(lo)
            elif hi > lo:
                with eng.Fori(lo, hi) as n:
                    body(n)

        x_rows = x.rearrange("(g p) c -> g p c", p=P)
        out_rows = out.rearrange("(g p) c -> g p c", p=P)
        o_rows = o_dram.rearrange("(g p) c -> g p c", p=P)
        o_heads = o_dram.rearrange("(b i p) (h d) -> b h p i d", b=B, p=P, d=D)

        block = ctx.enter_context(nc.Block())

        @block.sync
        def _(sp):
            sp.dma_start(w_f32[:], wqkv.rearrange("m (k p) n -> p m k n", p=P)).then_inc(weights_in, 16)
            sp.dma_start(tab_sb[:], table.rearrange("(o r) h -> o r h", o=1).to_broadcast([P, NBUCKET, H])
                         ).then_inc(table_in, 16)

            def load_head(g):
                wait(sp, xh_ready, g)
                sp.dma_start(xh[:], x_rows[g]).then_inc(xh_in, 16)

            def load_tail(g):
                if isinstance(g, int):
                    wait(sp, x2_ready, g)
                else:
                    sp.wait_ge(x2_ready, g)
                sp.dma_start(o_cur[:], o_rows[g]).then_inc(o_cur_in, 16)
                sp.dma_start(x_res[:], x_rows[g]).then_inc(x_res_in, 16)

            def store_out(g):
                sp.wait_ge(out_ready, g + 1)
                sp.dma_start(out_rows[g], out_sb[:]).then_inc(out_stored, 16)

            def spread_qk(h):
                rows = slice(D * h, D * h + D)
                sp.dma_start(q_pair[h][0:D, :], q_stage[rows, 0, :]).then_inc(qk_in[h], 16)
                sp.dma_start(q_pair[h][D:P, :], q_stage[rows, 1, :]).then_inc(qk_in[h], 16)
                sp.dma_start(k_twice[h][0:D, :, :], k_stage[rows, :, :]).then_inc(qk_in[h], 16)
                sp.dma_start(k_twice[h][D:P, :, :], k_stage[rows, :, :]).then_inc(qk_in[h], 16)

            def spread_v(h):
                sp.dma_start(v_head[h][:].rearrange("p i (a d) -> p i a d", a=2),
                             v_stage[:, :, h, :, :]).then_inc(v_in[h], 16)

            load_head(0)
            for dst, src in ((wp_sb, wp), (wr_sb, w_r), (wk_sb, w_k), (wv_sb, w_v)):
                sp.dma_start(dst[:], src.rearrange("(k p) n -> p k n", p=P)).then_inc(small_in, 16)
            sp.dma_start(bp_sb[:], bp.rearrange("(o c) -> o c", o=1).to_broadcast([P, C])).then_inc(small_in, 16)
            for m, mu in enumerate((mu_r, mu_k)):
                sp.dma_start(mu_sb[:, m, :], mu.rearrange("(k p) -> p k", p=P),
                             allow_slow_non_contiguous=True).then_inc(small_in, 16)
            rolled(sp, 1, HEAD_LEAD, load_head)

            sp.wait_ge(vec_setup, 7)
            sp.dma_start(band_dram.rearrange("h (p j) -> p h j", p=P), band_src[:]).then_inc(band_out, 16)
            sp.wait_ge(band_out, 16)
            shifted = band_dram[:, P - 1:P - 1 + P * (ROW - 1)].rearrange("h (p j) -> p h j", j=ROW - 1)
            sp.dma_start(band[:], shifted[:, :, 0:WIN]).then_inc(band_in, 16)

            sp.wait_ge(misc_free, HEAD_LEAD + len(NEXT_TASKS))
            for h in range(2):
                spread_qk(h)
                spread_v(h)

            for seg in segments:
                def body(n, seg=seg):
                    if seg.front:
                        load_tail(n - TAIL_LAG)
                    if seg.head:
                        load_head(n + HEAD_LEAD)
                    for h in range(2):
                        if seg.next:
                            if h == 0:
                                sp.wait_ge(misc_free, seg.index(n, "k1") + 1)
                            sp.wait_ge(scored, UNITS * n + NB * (h + 1))
                            spread_qk(h)
                            if h == 0:
                                sp.wait_ge(misc_free, seg.index(n, "v1") + 1)
                            sp.wait_ge(pv_done, UNITS * n + NB * (h + 1))
                            spread_v(h)
                        if h == 0 and seg.back:
                            store_out(n - TAIL_LAG - 1)
                rolled(sp, seg.lo, seg.hi, body)

            def last_tails(g):
                load_tail(g)
                store_out(g - 1)
            for h in range(2):
                sp.wait_ge(o_stored[h], 16 * N)
            rolled(sp, G - TAIL_LAG, G, last_tails)
            store_out(G - 1)
            sp.wait_ge(out_stored, 16 * G)

        @block.tensor
        def _(pe):
            def misc_open(index):
                pe.wait_ge(misc_free, index) if not isinstance(index, int) or index > 0 else None

            def head_transpose(g, index):
                pe.wait_ge(xh_ready, g + 1)
                misc_open(index)
                for k in range(KT):
                    last = pe.transpose(misc[:, k * P:(k + 1) * P], xh_norm[:, k * P:(k + 1) * P], ident[:])
                last.then_inc(misc_full, 1)

            def project_qk(which, half, pair, ring, index):
                misc_open(index)
                step = 0
                for k in range(KT):
                    for w, a in ((0, 0), (1, 0), (0, 1)):
                        last = pe.matmul(misc[:], w_split[:, w, which, k, bass.ds(pair, P)],
                                         xT[:, a, k, bass.ds(ring + half * 512, 512)],
                                         start=step == 0, stop=step == 3 * KT - 1)
                        step += 1
                last.then_inc(misc_full, 1)

            def project_v(half, pair, ring, index):
                misc_open(index)
                for i in range(4):
                    step = 0
                    for k in range(KT):
                        for w, a in ((0, 0), (1, 0), (0, 1)):
                            last = pe.matmul(misc[:, i * P:(i + 1) * P],
                                             xT[:, a, k, bass.ds(ring + (half * 4 + i) * P, P)],
                                             w_split[:, w, 2, k, bass.ds(pair, P)],
                                             start=step == 0, stop=step == 3 * KT - 1)
                            step += 1
                last.then_inc(misc_full, 1)

            def next_task(name, pair, ring, index):
                if name[0] == "v":
                    project_v(int(name[1]), pair, ring, index)
                else:
                    project_qk("qk".index(name[0]), int(name[1]), pair, ring, index)

            def tail_task(name, g, index):
                if name in ("ot0", "ot1"):
                    half = int(name[2])
                    if half == 0:
                        pe.wait_ge(o_cur_in, 16 * (g + 1))
                    misc_open(index)
                    for j in range(4):
                        c = half * 4 + j
                        last = pe.transpose(misc[:, j * P:(j + 1) * P], o_cur[:, c * P:(c + 1) * P], ident[:])
                elif name == "proj":
                    misc_open(index)
                    for c in range(H * D // P):
                        last = pe.matmul(misc[:, 0:C], oT[:, c, :], wp_sb[:, c, :], start=c == 0,
                                         stop=c == H * D // P - 1)
                elif name == "x2t":
                    pe.wait_ge(x2_normed, g + 1)
                    misc_open(index)
                    for k in range(KT):
                        last = pe.transpose(misc[:, k * P:(k + 1) * P], x2_norm[:, k * P:(k + 1) * P], ident[:])
                elif name == "rk":
                    pe.wait_ge(mixed_ready, 2 * KT * (g + 1))
                    misc_open(index)
                    for k in range(KT):
                        pe.matmul(misc[:, 0:C], mixed[:, 0, k, :], wr_sb[:, k, :], start=k == 0, stop=k == KT - 1)
                    for m in range(KT):
                        for k in range(KT):
                            last = pe.matmul(misc[:, C + m * P:C + (m + 1) * P], wk_sb[:, k, m * P:(m + 1) * P],
                                             mixed[:, 1, k, :], start=k == 0, stop=k == KT - 1)
                else:
                    pe.wait_ge(k_act_ready, g + 1)
                    misc_open(index)
                    for k in range(KT):
                        last = pe.matmul(misc[:, 0:C], k_act[:, k, :], wv_sb[:, k, :], start=k == 0,
                                         stop=k == KT - 1)
                last.then_inc(misc_full, 1)

            def score(n, u):
                (h, i), unit = head_block(u), UNITS * n + u
                if u % NB == 0:
                    pe.wait_ge(qk_in[h], 64 * (n + 1 + u // UNITS))
                wait(pe, exp_done, unit - 1)
                for c in range((i + 4) // 4):
                    cols = min(512, (i + 1) * P - c * 512)
                    for a in range(2):
                        last = pe.matmul(scores[:, u % 2, c * 512:c * 512 + cols], q_pair[h][:, i * P:(i + 1) * P],
                                         k_twice[h][:, a, c * 512:c * 512 + cols], start=a == 0, stop=a == 1)
                last.then_inc(scored, 1)

            def transpose_probs(n, u):
                pe.wait_ge(exp_done, UNITS * n + u + 1)
                for c, blocks in chunks(head_block(u)[1]):
                    k = CHUNK0[u] + c
                    wait(pe, lo_done, CHUNKS * n + k - 1)
                    for j in range(blocks):
                        s = 4 * c + j
                        last = pe.transpose(probsT_ps[k % 2][:, j, :], probs[:, u % 2, s * P:(s + 1) * P], ident[:])
                    last.then_inc(transposed, 1)

            def weigh_values(n, u):
                h, i = head_block(u)
                if u % NB == 0:
                    pe.wait_ge(v_in[h], 16 * (n + 1))
                pe.wait_ge(lo_done, CHUNKS * n + chunks_before(u + 1))
                wait(pe, parts_ready, UNITS * n + u)
                for s in range(i + 1):
                    for a in range(2):
                        last = pe.matmul(o_ps[:, 0:2 * D], probsT[:, u % 2, a, s, :], v_head[h][:, s, :],
                                         start=s == 0 and a == 0, stop=s == i and a == 1)
                last.then_inc(pv_done, 1)

            pe.wait_ge(ident_ready, 1)
            rolled(pe, 0, HEAD_LEAD, lambda g: head_transpose(g, g))
            pe.wait_ge(split_lo, 3)
            for k, name in enumerate(NEXT_TASKS):
                next_task(name, 0, 0, HEAD_LEAD + k)
            score(0, 0)
            score(0, 1)
            pe.wait_ge(small_in, 16 * 7)
            pe.wait_ge(vec_setup, 8)
            for seg in segments:
                def body(n, seg=seg):
                    pair, ring = (n + 1) % NPAIR * P, (n + 1) // NPAIR % 2 * T
                    if not isinstance(n, int):
                        pair, ring = pe.snap(pair), pe.snap(ring)
                    for u in range(UNITS):
                        transpose_probs(n, u)
                        if u + 2 < UNITS or seg.next:
                            score(n, u + 2)
                        name = seg.in_slot.get(u)
                        if name in NEXT_TASKS:
                            next_task(name, pair, ring, seg.index(n, name))
                        elif name in FRONT_TASKS or name in BACK_TASKS:
                            tail_task(name, seg.tail_block(n, name), seg.index(n, name))
                        elif name in HEAD_TASKS:
                            head_transpose(n + HEAD_LEAD, seg.index(n, name))
                        if u > 0 or not isinstance(n, int) or n > 0:
                            weigh_values(n, u - 1)
                rolled(pe, seg.lo, seg.hi, body)
            weigh_values(N - 1, UNITS - 1)

            def last_tails(g):
                for name in LAST_ORDER:
                    tail_task(name, g - (name in BACK_TASKS), last_index(g, name))
            rolled(pe, G - TAIL_LAG, G, last_tails)
            for name in BACK_TASKS:
                tail_task(name, G - 1, last_index(G, name))

        @block.scalar
        def _(act):
            def evacuate_high(dst, src, index):
                act.wait_ge(misc_full, index + 1)
                nc.scalar.copy(dst, src).then_inc(misc_hi, 1)

            def head_high(g, index):
                at = act.snap(g % (RING // P) * P) if not isinstance(g, int) else g % (RING // P) * P
                evacuate_high(xT[:, 0, :, bass.ds(at, P)], misc[:, 0:C].rearrange("p (k t) -> p k t", k=KT), index)

            def next_high(name, pairs_before, index):
                half = int(name[1])
                if name == "q0":
                    wait(act, qk_in[1], 64 * pairs_before)
                if name == "v0":
                    wait(act, v_in[1], 16 * pairs_before)
                if name[0] == "v":
                    evacuate_high(v_stage[:, 4 * half:4 * half + 4, :, 0, :],
                                  misc[:].rearrange("p (i h d) -> p i h d", i=4, h=2), index)
                else:
                    stage = q_stage if name[0] == "q" else k_stage
                    evacuate_high(stage[:, 0, half * 512:(half + 1) * 512], misc[:], index)

            def tail_step(name, g, index):
                if name in ("ot0", "ot1"):
                    half = int(name[2])
                    act.wait_ge(misc_full, index + 1)
                    nc.scalar.copy(oT[:, half * 4:half * 4 + 4, :],
                                   misc[:].rearrange("p (c t) -> p c t", c=4)).then_inc(misc_free, 1)
                elif name == "x2t":
                    act.wait_ge(misc_full, index + 1)
                    act.wait_ge(carried, KT * (g + 1))
                    nc.scalar.copy(x2T[:, :, 1:P + 1],
                                   misc[:, 0:C].rearrange("p (k t) -> p k t", k=KT)).then_inc(misc_free, 1)
                elif name == "rk":
                    act.wait_ge(misc_full, index + 1)
                    nc.scalar.activation(gate_exp[:], misc[:, 0:C], ACT.Exp, scale=-1.0).then_inc(gate_exped, 1)
                    nc.scalar.activation(k_relu[:], misc[:, C:2 * C].rearrange("p (k t) -> p k t", k=KT),
                                         ACT.Relu).then_inc(misc_free, 1)

            def exponential(n, u):
                unit, i = UNITS * n + u, head_block(u)[1]
                act.wait_ge(bias_ready, unit + 1)
                wait(act, transposed, CHUNKS * n + chunks_before(u - 1))
                wait(act, inv_ready, unit - 3)
                cols = (i + 1) * P
                nc.scalar.activation(probs[:, u % 2, 0:cols], scores[:, u % 2, 0:cols], ACT.Exp,
                                     bias=exp_bias[:, u % 4:u % 4 + 1], scale=score_unit[:],
                                     accum_out=row_sum[:, u % 4:u % 4 + 1]).then_inc(exp_done, 1)

            def high_parts(n, u):
                for c, blocks in chunks(head_block(u)[1]):
                    k = CHUNKS * n + CHUNK0[u] + c
                    act.wait_ge(transposed, k + 1)
                    if c == 0:
                        wait(act, pv_done, UNITS * n + u - 1)
                    nc.scalar.copy(probsT[:, u % 2, 0, 4 * c:4 * c + blocks, :],
                                   probsT_ps[(CHUNK0[u] + c) % 2][:, 0:blocks, :]).then_inc(hi_done, 1)

            def scale_output(n, u):
                unit = UNITS * n + u
                act.wait_ge(pv_done, unit + 1)
                act.wait_ge(inv_ready, unit + 1)
                wait(act, o_added, unit - 3)
                nc.scalar.activation(o_parts[:, u % 4, :], o_ps[:, 0:2 * D], ACT.Copy,
                                     scale=inv_sum[:, u % 4:u % 4 + 1]).then_inc(parts_ready, 1)

            rolled(act, 0, HEAD_LEAD, lambda g: head_high(g, g))
            for k, name in enumerate(NEXT_TASKS):
                next_high(name, 0, HEAD_LEAD + k)
            exponential(0, 0)
            for seg in segments:
                def body(n, seg=seg):
                    for u in range(UNITS):
                        if u > 1 or not isinstance(n, int) or n > 0:
                            scale_output(n, u - 2)
                        high_parts(n, u)
                        if u + 1 < UNITS or seg.next:
                            exponential(n, u + 1)
                        name = seg.in_slot.get(u)
                        if name in NEXT_TASKS:
                            next_high(name, n + 1, seg.index(n, name))
                        elif name in FRONT_TASKS or name in BACK_TASKS:
                            tail_step(name, seg.tail_block(n, name), seg.index(n, name))
                        elif name in HEAD_TASKS:
                            head_high(n + HEAD_LEAD, seg.index(n, name))
                rolled(act, seg.lo, seg.hi, body)
            scale_output(N - 1, UNITS - 2)
            scale_output(N - 1, UNITS - 1)

            def last_tails(g):
                for name in LAST_ORDER:
                    tail_step(name, g - (name in BACK_TASKS), last_index(g, name))
            rolled(act, G - TAIL_LAG, G, last_tails)
            for name in BACK_TASKS:
                tail_step(name, G - 1, last_index(G, name))

        @block.vector
        def _(dve):
            def statistics(name, src, g, stats_sem, aggr_sem, ready_sem, ready, used_sem):
                bn, mv = ln_bufs[name][:2]
                wait(dve, ready_sem, ready)
                dve.bn_stats(bn[:], src).then_inc(stats_sem, 1)
                dve.wait_ge(stats_sem, g + 1)
                wait(dve, used_sem, g)
                plain(dve)
                dve.bn_aggr(mv[:], bn[:]).then_inc(aggr_sem, 1)

            def evacuate_low(dst, src, high, hi_count):
                dve.wait_ge(misc_hi, hi_count)
                dve.tensor_tensor(dst, src, high, ALU.subtract).then_inc(misc_free, 1)

            def head_low(g, hi_count):
                at = dve.snap(g % (RING // P) * P) if not isinstance(g, int) else g % (RING // P) * P
                evacuate_low(xT[:, 1, :, bass.ds(at, P)], misc[:, 0:C].rearrange("p (k t) -> p k t", k=KT),
                             xT[:, 0, :, bass.ds(at, P)], hi_count)

            def next_low(name, hi_count):
                half = int(name[1])
                if name[0] == "v":
                    evacuate_low(v_stage[:, 4 * half:4 * half + 4, :, 1, :],
                                 misc[:].rearrange("p (i h d) -> p i h d", i=4, h=2),
                                 v_stage[:, 4 * half:4 * half + 4, :, 0, :], hi_count)
                else:
                    stage = q_stage if name[0] == "q" else k_stage
                    cols = slice(half * 512, (half + 1) * 512)
                    evacuate_low(stage[:, 1, cols], misc[:], stage[:, 0, cols], hi_count)

            def tail_step(name, g, index):
                if name == "proj":
                    dve.wait_ge(misc_full, index + 1)
                    wait(dve, y_normed, g)
                    dve.tensor_tensor(y[:], misc[:, 0:C], bp_sb[:], ALU.add).then_inc(misc_free, 1)
                    statistics("y", y[:], g, y_stats, y_aggr, misc_free, index + 1, y_normed)
                elif name == "x2stats":
                    statistics("x2", x2[:], g, x2_stats, x2_aggr, x2_ready, g + 1, x2_normed)
                elif name == "mix":
                    dve.wait_ge(delta_ready, g + 1)
                    for m in range(2):
                        for k in range(KT):
                            dve.scalar_tensor_tensor(mixed[:, m, k, :], delta[:, k, :], mu_sb[:, m, k:k + 1],
                                                     x2T[:, k, 0:P], ALU.mult, ALU.add).then_inc(mixed_ready, 1)
                elif name == "gate":
                    dve.wait_ge(den_ready, g + 1)
                    dve.reciprocal(gate[:], gate_den[:]).then_inc(gate_ready, 1)
                elif name == "ffn":
                    dve.wait_ge(misc_full, index + 1)
                    dve.wait_ge(gate_ready, g + 1)
                    wait(dve, z_normed, g)
                    dve.tensor_tensor(z[:], misc[:, 0:C], gate[:], ALU.mult).then_inc(misc_free, 1)
                    statistics("z", z[:], g, z_stats, z_aggr, misc_free, index + 1, z_normed)

            def row_bias(n, u):
                (h, i), unit = head_block(u), UNITS * n + u
                cols = (i + 1) * P
                pair_count = n + 1 + u // UNITS
                if u % NB == 0:
                    dve.wait_ge(bias_row_in[h], pair_count)
                dve.wait_ge(scored, unit + 1)
                plain(dve)
                dve.tensor_tensor_reduce(out=scores[:, u % 2, 0:cols], in0=scores[:, u % 2, 0:cols],
                                         in1=bias_row[h][:, T - cols:T], scale=1.0, scalar=-3.4e38, op0=ALU.add,
                                         op1=ALU.max, accum_out=row_max[:, u % 4:u % 4 + 1]).then_inc(max_ready, 1)
                dve.wait_ge(max_ready, unit + 1)
                wait(dve, exp_done, unit - 3)
                dve.tensor_scalar(exp_bias[:, u % 4:u % 4 + 1], row_max[:, u % 4:u % 4 + 1], neg_unit[:, 0:1],
                                  P_SHIFT, ALU.mult, ALU.add).then_inc(bias_ready, 1)

            def low_parts(n, u):
                for c, blocks in chunks(head_block(u)[1]):
                    k = CHUNKS * n + CHUNK0[u] + c
                    dve.wait_ge(hi_done, k + 1)
                    dve.tensor_tensor(probsT[:, u % 2, 1, 4 * c:4 * c + blocks, :],
                                      probsT_ps[(CHUNK0[u] + c) % 2][:, 0:blocks, :],
                                      probsT[:, u % 2, 0, 4 * c:4 * c + blocks, :], ALU.subtract).then_inc(lo_done, 1)

            def invert_sum(n, u):
                unit = UNITS * n + u
                dve.wait_ge(exp_done, unit + 1)
                wait(dve, parts_ready, unit - 3)
                dve.reciprocal(inv_sum[:, u % 4:u % 4 + 1], row_sum[:, u % 4:u % 4 + 1]).then_inc(inv_ready, 1)

            def head_stats(g):
                statistics("xh", xh[:], g, xh_stats, xh_aggr, xh_in, 16 * (g + 1), xh_ready)

            dve.wait_ge(weights_in, 16)
            for m in range(3):
                last = dve.tensor_reduce(top[:, m:m + 1], w_f32[:, m, :, :], AX.XY, ALU.max,
                                         apply_absolute_value=True)
            last.then_inc(top_ready, 1)
            dve.wait_ge(top_reduced, 1)
            dve.tensor_scalar(top_all[:], top_all[:], 2.0 ** -40, None, ALU.max).then_inc(vec_setup, 1)
            dve.wait_ge(vec_setup, 1)
            dve.tensor_scalar(pow2[:].bitcast(I32), top_all[:].bitcast(I32), 0x7F800000, None,
                              ALU.bitwise_and).then_inc(vec_setup, 1)
            dve.wait_ge(vec_setup, 2)
            dve.reciprocal(inv2[:], pow2[:]).then_inc(vec_setup, 1)
            dve.wait_ge(vec_setup, 3)
            dve.tensor_scalar(w_scale[:], inv2[:], W_TOP, None, ALU.mult)
            dve.tensor_scalar(score_unit[:], pow2[:, 0:1], pow2[:, 1:2], D ** -0.5 / W_TOP ** 2, ALU.mult, ALU.mult)
            dve.tensor_scalar(neg_unit[:], pow2[:, 0:1], pow2[:, 1:2], -D ** -0.5 / W_TOP ** 2, ALU.mult, ALU.mult)
            dve.tensor_scalar(band_unit[:], inv2[:, 0:1], inv2[:, 1:2], D ** 0.5 * W_TOP ** 2,
                              ALU.mult, ALU.mult).then_inc(vec_setup, 1)
            dve.wait_ge(vec_setup, 4)
            for m in range(3):
                dve.tensor_scalar(w_split[:, 0, m], w_f32[:, m], w_scale[:, m:m + 1], None,
                                  ALU.mult).then_inc(split_hi, 1)
            for m in range(3):
                dve.wait_ge(split_hi, m + 1)
                dve.scalar_tensor_tensor(w_split[:, 1, m], w_f32[:, m], w_scale[:, m:m + 1], w_split[:, 0, m],
                                         ALU.mult, ALU.subtract).then_inc(split_lo, 1)
            dve.wait_ge(table_in, 16)
            dve.memset(band_src[:, :, 0:P], 0.0)
            dve.memset(band_src[:, :, WIN:ROW], MASKED).then_inc(vec_setup, 1)
            dve.tensor_tensor(band_src[:, :, P:WIN], tab_sb[:, 1:1 + MAX_REL, :].rearrange("p r h -> p h r"),
                              tab_sb[:, 0:1, :].rearrange("p r h -> p h r").to_broadcast([P, H, MAX_REL]),
                              ALU.subtract).then_inc(vec_setup, 1)
            dve.wait_ge(vec_setup, 6)
            dve.tensor_scalar(band_src[:, :, P:WIN], band_src[:, :, P:WIN], band_unit[:, 0:1], None,
                              ALU.mult).then_inc(vec_setup, 1)
            dve.wait_ge(small_in, 16 * 7)
            dve.tensor_scalar(wp_sb[:], wp_sb[:], pow2[:, 2:3], 1.0 / W_TOP, ALU.mult, ALU.mult).then_inc(vec_setup, 1)

            def prologue_head(g):
                head_stats(g)
                head_low(g, g + 1)
            rolled(dve, 0, HEAD_LEAD, prologue_head)
            for k, name in enumerate(NEXT_TASKS):
                next_low(name, HEAD_LEAD + k + 1)
            row_bias(0, 0)
            row_bias(0, 1)

            two_part = {**NEXT_TASKS, **HEAD_TASKS}
            hi_base = HEAD_LEAD + len(NEXT_TASKS)
            for seg in segments:
                split = [name for name in seg.order if name in two_part]

                def body(n, seg=seg, split=split, hi_base=hi_base):
                    for u in range(UNITS):
                        low_parts(n, u)
                        invert_sum(n, u)
                        if u + 2 < UNITS or seg.next:
                            row_bias(n, u + 2)
                        name = seg.in_slot.get(u)
                        if name in split:
                            count = hi_base + len(split) * (n - seg.lo) + split.index(name) + 1
                            if name in NEXT_TASKS:
                                next_low(name, count)
                            else:
                                head_low(n + HEAD_LEAD, count)
                        elif name in ("proj", "ffn"):
                            tail_step(name, seg.tail_block(n, name), seg.index(n, name))
                        step = VEC_STEPS.get(u)
                        if step and seg.has(step):
                            if step == "head":
                                head_stats(n + HEAD_LEAD)
                            else:
                                tail_step(step, seg.tail_block(n, step), None)
                rolled(dve, seg.lo, seg.hi, body)
                hi_base += len(split) * (seg.hi - seg.lo)

            def last_tails(g):
                tail_step("mix", g - 1, None)
                tail_step("proj", g, last_index(g, "proj"))
                tail_step("x2stats", g, None)
                tail_step("gate", g - 1, None)
                tail_step("ffn", g - 1, last_index(g, "ffn"))
            rolled(dve, G - TAIL_LAG, G, last_tails)
            tail_step("mix", G - 1, None)
            tail_step("gate", G - 1, None)
            tail_step("ffn", G - 1, last_index(G, "ffn"))

        @block.gpsimd
        def _(pool):
            def normalise(name, dst, src, g, aggr_sem, pool_sem, done_sem, dst_free):
                _, mv, var, a, b, r = ln_bufs[name]
                count = LN_OPS * g
                wait(pool, done_sem, g)
                pool.wait_ge(aggr_sem, g + 1)
                plain(pool)
                pool.tensor_scalar(var[:], mv[:, 1:2], EPS, None, ALU.add).then_inc(pool_sem, 1)
                pool.wait_ge(pool_sem, count + 1)
                plain(pool)
                pool.tensor_scalar(r[:, 0:1].bitcast(I32), var[:].bitcast(I32), -0.5, RSQRT_SEED,
                                   ALU.mult, ALU.add).then_inc(pool_sem, 1)
                for k in range(NEWTON):
                    pool.wait_ge(pool_sem, count + 3 * k + 2)
                    plain(pool)
                    pool.tensor_scalar(a[:], r[:, k:k + 1], r[:, k:k + 1], var[:], ALU.mult,
                                       ALU.mult).then_inc(pool_sem, 1)
                    pool.wait_ge(pool_sem, count + 3 * k + 3)
                    plain(pool)
                    pool.tensor_scalar(b[:], a[:], -0.5, 1.5, ALU.mult, ALU.add).then_inc(pool_sem, 1)
                    pool.wait_ge(pool_sem, count + 3 * k + 4)
                    pool.tensor_tensor(r[:, k + 1:k + 2], r[:, k:k + 1], b[:], ALU.mult).then_inc(pool_sem, 1)
                pool.wait_ge(pool_sem, count + LN_OPS)
                wait(pool, *dst_free)
                plain(pool)
                pool.tensor_scalar(dst, src, mv[:, 0:1], r[:, NEWTON:NEWTON + 1], ALU.subtract,
                                   ALU.mult).then_inc(done_sem, 1)

            def add_parts(n, u):
                (h, i), unit = head_block(u), UNITS * n + u
                pool.wait_ge(parts_ready, unit + 1)
                if u % NB == 0:
                    wait(pool, o_stored[h], 16 * n if u >= 0 else 16 * (n - 1))
                pool.tensor_tensor(o_stage[h][:, i, :], o_parts[:, u % 4, 0:D], o_parts[:, u % 4, D:2 * D],
                                   ALU.add).then_inc(o_added, 1)

            def set_bias_row(n, h, pair):
                wait(pool, max_ready, UNITS * (n - 1) + NB * (h + 1))
                pool.tensor_copy(bias_row[h][:, T - WIN:T], band[:, bass.ds(2 * pair + h, 1), :].rearrange(
                    "p o j -> p (o j)")).then_inc(bias_row_in[h], 1)

            def store_head(n, h, b, pair):
                pool.wait_ge(o_added, UNITS * n + NB * (h + 1))
                pool.dma_start(o_heads[b, pair * 2 + h], o_stage[h][:]).then_inc(o_stored[h], 16)

            def tail_step(name, g):
                if name == "x2":
                    normalise("y", y_norm[:], y[:], g, y_aggr, y_pool, y_normed, (x2_ready, g))
                    pool.wait_ge(y_normed, g + 1)
                    pool.wait_ge(x_res_in, 16 * (g + 1))
                    wait(pool, x2_kept, g)
                    pool.tensor_tensor(x2[:], x_res[:], y_norm[:], ALU.add).then_inc(x2_ready, 1)
                elif name == "x2_norm":
                    normalise("x2", x2_norm[:], x2[:], g, x2_aggr, x2_pool, x2_normed, (mixed_ready, 2 * KT * g))
                    for k in range(KT):
                        pool.tensor_tensor(x2T[:, k, 0:1], x2T[:, k, P:P + 1], keep_carry[:, bass.ds(g, 1)],
                                           ALU.mult).then_inc(carried, 1)
                elif name == "delta":
                    pool.tensor_tensor(delta[:], x2T[:, :, 1:P + 1], x2T[:, :, 0:P],
                                       ALU.subtract).then_inc(delta_ready, 1)
                elif name == "act":
                    pool.wait_ge(gate_exped, g + 1)
                    wait(pool, gate_ready, g)
                    plain(pool)
                    pool.tensor_scalar(gate_den[:], gate_exp[:], 1.0, None, ALU.add).then_inc(den_ready, 1)
                    pool.tensor_tensor(k_act[:], k_relu[:], k_relu[:], ALU.mult).then_inc(k_act_ready, 1)
                elif name == "keep":
                    pool.wait_ge(x2_ready, g + 1)
                    wait(pool, out_ready, g)
                    plain(pool)
                    pool.tensor_copy(x2_keep[:], x2[:]).then_inc(x2_kept, 1)
                else:
                    normalise("z", z_norm[:], z[:], g, z_aggr, z_pool, z_normed, (out_ready, g))
                    pool.wait_ge(z_normed, g + 1)
                    pool.wait_ge(x2_kept, g + 1)
                    wait(pool, out_stored, 16 * g)
                    pool.tensor_tensor(out_sb[:], x2_keep[:], z_norm[:], ALU.add).then_inc(out_ready, 1)

            pool.memset(ident[:], 0.0).then_inc(pool_setup, 1)
            pool.wait_ge(pool_setup, 1)
            pool.affine_select(out=ident[:], in_=ident[:], compare_op=ALU.not_equal, fill=1.0, base=0,
                               pattern=[[-1, P]], channel_multiplier=1).then_inc(ident_ready, 1)
            pool.memset(keep_carry[:], 1.0).then_inc(pool_setup, 1)
            pool.memset(x2T[:], 0.0).then_inc(pool_setup, 1)
            for h in range(2):
                pool.memset(bias_row[h][:, 0:T - WIN], 0.0).then_inc(pool_setup, 1)
            pool.wait_ge(pool_setup, 5)
            pool.memset(keep_carry[:].rearrange("p (b i) -> p b i", i=NB)[:, :, 0:1], 0.0).then_inc(pool_setup, 1)
            pool.wait_ge(top_ready, 1)
            pool.partition_all_reduce(top_all[:], top[:], P, bass.bass_isa.ReduceOp.max).then_inc(top_reduced, 1)
            pool.wait_ge(pool_setup, 6)

            rolled(pool, 0, HEAD_LEAD, lambda g: normalise("xh", xh_norm[:], xh[:], g, xh_aggr, xh_pool, xh_ready,
                                                           (misc_free, g)))
            pool.wait_ge(band_in, 16)
            set_bias_row(0, 0, 0)
            set_bias_row(0, 1, 0)
            for seg in segments:
                def body(n, seg=seg):
                    g = n - TAIL_LAG
                    b, pair = (n // NPAIR, n % NPAIR) if isinstance(n, int) else (pool.snap(n // NPAIR),
                                                                                pool.snap(n % NPAIR))
                    next_pair = (n + 1) % NPAIR if isinstance(n, int) else pool.snap((n + 1) % NPAIR)
                    for u in range(UNITS):
                        if u > 1 or not isinstance(n, int) or n > 0:
                            add_parts(n, u - 2)
                        if u == 1 and (not isinstance(n, int) or n > 0):
                            if isinstance(n, int):
                                store_head(n - 1, 1, (n - 1) // NPAIR, (n - 1) % NPAIR)
                            else:
                                store_head(n - 1, 1, pool.snap((n - 1) // NPAIR), pool.snap((n - 1) % NPAIR))
                        if u == NB + 1:
                            store_head(n, 0, b, pair)
                            if seg.next:
                                set_bias_row(n + 1, 0, next_pair)
                        if u == 0 and (not isinstance(n, int) or n > 0):
                            set_bias_row(n, 1, pair)
                        step = POOL_STEPS.get(u)
                        if step == "head" and seg.head:
                            normalise("xh", xh_norm[:], xh[:], n + HEAD_LEAD, xh_aggr, xh_pool, xh_ready,
                                      (misc_free, seg.index(n, "q0")))
                        elif step and step != "head" and seg.has(step):
                            if step == "delta":
                                pool.wait_ge(misc_free, seg.index(n, "x2t") + 1)
                            if step == "act":
                                pool.wait_ge(misc_free, seg.index(n, "rk") + 1)
                            tail_step(step, seg.tail_block(n, step))
                            if step == "x2_norm":
                                tail_step("keep", seg.tail_block(n, step))
                rolled(pool, seg.lo, seg.hi, body)
            add_parts(N - 1, UNITS - 2)
            add_parts(N - 1, UNITS - 1)
            store_head(N - 1, 1, B - 1, NPAIR - 1)

            def last_tails(g):
                pool.wait_ge(misc_free, last_index(g, "x2t") + 1)
                tail_step("delta", g - 1)
                tail_step("x2", g)
                pool.wait_ge(misc_free, last_index(g, "rk") + 1)
                tail_step("act", g - 1)
                tail_step("x2_norm", g)
                tail_step("out", g - 1)
                tail_step("keep", g)
            rolled(pool, G - TAIL_LAG, G, last_tails)
            pool.wait_ge(misc_free, last_index(G, "x2t") + 1)
            tail_step("delta", G - 1)
            pool.wait_ge(misc_free, last_index(G, "rk") + 1)
            tail_step("act", G - 1)
            tail_step("out", G - 1)


def kernel(**inputs):
    import numpy as np
    import concourse.bacc as bacc
    from concourse.bass_utils import run_bass_kernel_spmd

    a = {k.split("_", 1)[1]: np.asarray(v) for k, v in inputs.items()}
    heads_last = [a[f"attn_{w}"].transpose(1, 0, 2).reshape(C, H * D) for w in ("Wq", "Wk", "Wv")]
    arrays = {
        "x": a["attn_x"].reshape(B * T, C),
        "wqkv": np.stack(heads_last),
        "wp": a["attn_Wp"],
        "bp": a["attn_bp"],
        "table": a["attn_rel_table"],
        "w_r": a["ffn_W_r"].T,
        "w_k": a["ffn_W_k"].T,
        "w_v": a["ffn_W_v"].T,
        "mu_r": a["ffn_mu_r"],
        "mu_k": a["ffn_mu_k"],
    }
    arrays = {k: np.ascontiguousarray(v) for k, v in arrays.items()}
    nc = bacc.Bacc("TRN2", target_bir_lowering=False, num_devices=1)
    args = [nc.dram_tensor(k, v.shape, mybir.dt.from_np(v.dtype), kind="ExternalInput").ap()
            for k, v in arrays.items()]
    out = nc.dram_tensor("out", [B * T, C], F32, kind="ExternalOutput").ap()
    build(nc, *args, out)
    r = run_bass_kernel_spmd(nc, [arrays], core_ids=[0])
    return r.results[0]["out"].reshape(B, T, C)
```

```python
from contextlib import ExitStack
from math import log

import concourse.bass as bass
from concourse import mybir

P = 128
B, T, C, H, D = 8, 1024, 256, 16, 64
NBUCKET, MAX_REL = 33, 16
KT = C // P
NB = T // P
NPAIR = H // 2
N = B * NPAIR
G = B * NB
UNITS = 2 * NB
HEAD_LEAD, TAIL_LAG = NB + 1, NPAIR + 1
KEPT_FROM = G - TAIL_LAG - 1
RING = 2 * T
WIN = P + MAX_REL
ROW = WIN + P
MASKED = -3.0e38
FIRST_CHUNK, SECOND_CHUNK = slice(0, 1), slice(1, 2)
EPS = 1e-5
W_TOP = 64.0
P_SHIFT = 14 * log(2.0)
RSQRT_SEED = float(0x5F3759DF) - 0.5 * (2.0 ** 31 + 2.0 ** 23)
NEWTON = 3
LN_OPS = 2 + 2 * NEWTON

ALU = mybir.AluOpType
ACT = mybir.ActivationFunctionType
AX = mybir.AxisListType
F32, F16, I32 = mybir.dt.float32, mybir.dt.float16, mybir.dt.int32

NEXT_TASKS = {"q0": 0, "q1": 2, "k0": 4, "k1": 6, "v0": 8, "v1": 12}
FRONT_TASKS = {"ot0": 3, "ot1": 5, "proj": 15}
BACK_TASKS = {"x2t": 7, "rk": 10, "ffn": 13}
HEAD_TASKS = {"xt": 14}
LAST_ORDER = ["x2t", "rk", "ot0", "ot1", "ffn", "proj"]
VEC_STEPS = {8: "mix", 11: "gate0", 12: "gate1"}
VEC_STATS = {3: "x2", 5: "xh", 14: "z"}
VEC_AGGR = {0: "y", 3: "x2", 5: "xh", 14: "z"}
POOL_STEPS = {0: "x2", 4: "x2_norm", 7: "delta", 8: "head", 10: "act", 14: "out"}

ORDER = [0, 7, 1, 6, 2, 5, 3, 4]


class Task:

    def __init__(self, bank, before, before_in_bank):
        self.bank, self.before, self.opens = bank, before, before_in_bank
        self.full = before + 1
        self.done = before_in_bank + 1


class Tasks:

    def __init__(self, lo, hi, order, counts):
        self.lo, self.hi, self.order, self.counts = lo, hi, order, counts
        self.banks = [k % 2 for k in range(len(order))]
        steps = [len(order), self.banks.count(0), self.banks.count(1)]
        self.steps = steps
        self.end = [c + s * (hi - lo) for c, s in zip(counts, steps)]

    def task(self, n, name):
        at = self.order.index(name)
        bank = self.banks[at]
        return Task(bank, self.counts[0] + self.steps[0] * (n - self.lo) + at,
                    self.counts[1 + bank] + self.steps[1 + bank] * (n - self.lo) + self.banks[:at].count(bank))


class Segment(Tasks):

    def __init__(self, lo, hi, counts):
        self.next = lo < N - 1
        self.head = lo < G - HEAD_LEAD
        self.front = lo >= TAIL_LAG
        self.back = lo >= TAIL_LAG + 1
        slots = {**(NEXT_TASKS if self.next else {}), **(FRONT_TASKS if self.front else {}),
                 **(BACK_TASKS if self.back else {}), **(HEAD_TASKS if self.head else {})}
        super().__init__(lo, hi, sorted(slots, key=slots.get), counts)
        self.in_slot = {slots[name]: name for name in self.order}

    def tail_block(self, n, name):
        return n - TAIL_LAG - (name not in FRONT_TASKS)

    def step_block(self, n, name):
        return n + HEAD_LEAD if name in ("head", "xh") else self.tail_block(n, name)

    def has(self, name):
        return self.head if name in ("head", "xh") else self.back


def plan():
    first = Tasks(0, 1, list(NEXT_TASKS), [HEAD_LEAD, HEAD_LEAD, 0])
    segments, counts = [], first.end
    for lo, hi in ((0, 1), (1, TAIL_LAG), (TAIL_LAG, TAIL_LAG + 1),
                   (TAIL_LAG + 1, TAIL_LAG + 2), (TAIL_LAG + 2, G - HEAD_LEAD), (G - HEAD_LEAD, N - 1), (N - 1, N)):
        segments.append(Segment(lo, hi, counts))
        counts = segments[-1].end
    lead = Tasks(G - TAIL_LAG, G - TAIL_LAG + 1, list(FRONT_TASKS), counts)
    closing = Tasks(G - TAIL_LAG, G - 1, LAST_ORDER, lead.end)
    return first, segments, lead, closing, Tasks(G - 1, G + 1, list(BACK_TASKS), closing.end)


def chunks(i):
    return [(c, min(4, i + 1 - 4 * c)) for c in range((i + 4) // 4)]


def head_block(u):
    return u % UNITS // NB, ORDER[u % NB]


CHUNK0 = [sum(len(chunks(head_block(k)[1])) for k in range(u)) for u in range(UNITS + 1)]
CHUNKS = CHUNK0[UNITS]


def chunks_before(u):
    return CHUNKS * (u // UNITS) + CHUNK0[u % UNITS]


def build(nc, x, wqkv, wp, bp, table, w_r, w_k, w_v, mu_r, mu_k, out):
    first, segments, lead, closing, final = plan()
    assert all((i >= 4) == k % 2 for k, i in enumerate(ORDER))
    with ExitStack() as ctx:
        def sb(name, shape, dt):
            return ctx.enter_context(nc.sbuf_tensor(name, shape, dt))

        def ps(name, shape):
            return ctx.enter_context(nc.psum_tensor(name, shape, F32))

        def sem(name):
            return ctx.enter_context(nc.semaphore(name))

        o_dram = nc.dram_tensor("o_scratch", [B * T, H * D], F32, kind="Internal").ap()
        band_dram = nc.dram_tensor("band_scratch", [H, P * ROW], F32, kind="Internal").ap()

        ident = sb("ident", [P, P], F32)
        w_f32 = sb("w_f32", [P, 3, KT, H * D], F32)
        w_split = sb("w_split", [P, 2, 3, KT, H * D], F16)
        wp_sb = sb("wp_sb", [P, H * D // P, C], F32)
        wr_sb = sb("wr_sb", [P, KT, C], F32)
        wk_sb = sb("wk_sb", [P, KT, C], F32)
        wv_sb = sb("wv_sb", [P, KT, C], F32)
        bp_sb = sb("bp_sb", [P, C], F32)
        mu_sb = sb("mu_sb", [P, 2, KT], F32)
        tab_sb = sb("tab_sb", [P, NBUCKET, H], F32)
        band_src = sb("band_src", [P, H, ROW], F32)
        band = sb("band", [P, H, WIN], F32)
        top = sb("top", [P, 3], F32)
        top_all = sb("top_all", [P, 3], F32)
        pow2 = sb("pow2", [P, 3], F32)
        inv2 = sb("inv2", [P, 3], F32)
        w_scale = sb("w_scale", [P, 3], F32)
        score_unit = sb("score_unit", [P, 1], F32)
        neg_unit = sb("neg_unit", [P, 1], F32)
        band_unit = sb("band_unit", [P, 1], F32)
        keep_carry = sb("keep_carry", [P, G], F32)

        xh = sb("xh", [P, C], F32)
        xh_norm = sb("xh_norm", [P, C], F32)
        xT = sb("xT", [P, 2, KT, RING], F16)

        q_stage = sb("q_stage", [P, 2, T], F16)
        k_stage = sb("k_stage", [P, 2, T], F16)
        v_stage = sb("v_stage", [P, NB, 2, 2, D], F16)
        q_pair = [sb(f"q_pair{h}", [P, T], F16) for h in range(2)]
        k_twice = [sb(f"k_twice{h}", [P, 2, T], F16) for h in range(2)]
        v_head = [sb(f"v_head{h}", [P, NB, 2 * D], F16) for h in range(2)]

        probs = sb("probs", [P, 2, T], F32)
        probsT = sb("probsT", [P, 2, 2, NB, P], F16)
        row_max = sb("row_max", [P, 4], F32)
        bias_row = [sb(f"bias_row{h}", [P, T], F32) for h in range(2)]
        exp_bias = sb("exp_bias", [P, 4], F32)
        row_sum = sb("row_sum", [P, 4], F32)
        inv_sum = sb("inv_sum", [P, 4], F32)
        o_parts = sb("o_parts", [P, 4, 2 * D], F32)
        o_stage = [sb(f"o_stage{h}", [P, NB, D], F32) for h in range(2)]

        o_cur = sb("o_cur", [P, H * D], F32)
        oT = sb("oT", [P, H * D // P, P], F32)
        x_res = sb("x_res", [P, C], F32)
        y = sb("y", [P, C], F32)
        y_norm = sb("y_norm", [P, C], F32)
        x2 = sb("x2", [P, C], F32)
        x2_keep = sb("x2_keep", [P, C], F32)
        x2_norm = sb("x2_norm", [P, C], F32)
        x2T = sb("x2T", [P, KT, P + 1], F32)
        delta = sb("delta", [P, KT, P], F32)
        mixed = sb("mixed", [P, 2, KT, P], F32)
        gate_exp = sb("gate_exp", [P, C], F32)
        gate_den = sb("gate_den", [P, C], F32)
        gate = sb("gate", [P, C], F32)
        k_relu = sb("k_relu", [P, KT, P], F32)
        k_act = sb("k_act", [P, KT, P], F32)
        z = sb("z", [P, C], F32)
        z_norm = sb("z_norm", [P, C], F32)
        out_sb = sb("out_sb", [P, C], F32)

        scores = [ps("scores_small", [P, T // 2]), ps("scores_large", [P, T])]
        probsT_ps = [ps(f"probsT_ps{k}", [P, 4, P]) for k in range(2)]
        o_ps = ps("o_ps", [P, 512])
        misc_banks = [ps(f"misc{k}", [P, 512]) for k in range(2)]

        weights_in, small_in = sem("weights_in"), sem("small_in")
        table_in, band_out, band_in = sem("table_in"), sem("band_out"), sem("band_in")
        pool_setup, top_ready, top_reduced = sem("pool_setup"), sem("top_ready"), sem("top_reduced")
        vec_setup, split_hi, split_lo = sem("vec_setup"), sem("split_hi"), sem("split_lo")
        ident_ready = sem("ident_ready")
        misc_full, misc_hi = sem("misc_full"), sem("misc_hi")
        misc_free = [sem(f"misc_free{k}") for k in range(2)]
        xh_odd_in = sem("xh_odd_in")
        xh_in, xh_stats, xh_aggr = sem("xh_in"), sem("xh_stats"), sem("xh_aggr")
        xh_root, xh_ready = sem("xh_root"), sem("xh_ready")
        qk_in = [sem(f"qk_in{h}") for h in range(2)]
        v_in = [sem(f"v_in{h}") for h in range(2)]
        o_stored = [sem(f"o_stored{h}") for h in range(2)]
        scored, max_ready = sem("scored"), sem("max_ready")
        bias_row_in = [sem(f"bias_row_in{h}") for h in range(2)]
        bias_ready, exp_done, transposed = sem("bias_ready"), sem("exp_done"), sem("transposed")
        hi_done, lo_done, pv_done = sem("hi_done"), sem("lo_done"), sem("pv_done")
        inv_ready, parts_ready, o_added = sem("inv_ready"), sem("parts_ready"), sem("o_added")
        o_cur_in, x_res_in = sem("o_cur_in"), sem("x_res_in")
        y_stats, y_aggr, y_root, y_normed = sem("y_stats"), sem("y_aggr"), sem("y_root"), sem("y_normed")
        x2_ready, x2_stats, x2_aggr, x2_root, x2_normed = (
            sem("x2_ready"), sem("x2_stats"), sem("x2_aggr"), sem("x2_root"), sem("x2_normed"))
        carried, delta_ready, mixed_ready = sem("carried"), sem("delta_ready"), sem("mixed_ready")
        gate_exped, den_ready, gate_ready, k_act_ready = (
            sem("gate_exped"), sem("den_ready"), sem("gate_ready"), sem("k_act_ready"))
        z_stats, z_aggr, z_root, z_normed = sem("z_stats"), sem("z_aggr"), sem("z_root"), sem("z_normed")
        out_ready, out_stored, x2_kept = sem("out_ready"), sem("out_stored"), sem("x2_kept")

        ln_bufs = {}
        for name in ("xh", "y", "x2", "z"):
            ln_bufs[name] = (sb(f"{name}_bn", [P, 6], F32), sb(f"{name}_mv", [P, 2], F32),
                             sb(f"{name}_half_var", [P, 1], F32), sb(f"{name}_a", [P, 1], F32),
                             sb(f"{name}_r", [P, NEWTON + 1], F32))

        def wait(eng, semaphore, value):
            if isinstance(value, int) and value <= 0:
                return
            eng.wait_ge(semaphore, value)

        def evacuated(eng, task):
            eng.wait_ge(misc_free[task.bank], task.done)

        def plain(eng):
            eng.nop(nofuse=True)

        def rolled(eng, lo, hi, body):
            if lo == 0:
                body(0)
                lo = 1
            if hi - lo == 1:
                body(lo)
            elif hi > lo:
                with eng.Fori(lo, hi) as n:
                    body(n)

        def normalise(eng, name, dst, src, g, aggr_sem, root_sem, done_sem, dst_free):
            _, mv, half_var, a, r = ln_bufs[name]
            count = LN_OPS * g
            wait(eng, done_sem, g)
            eng.wait_ge(aggr_sem, g + 1)
            plain(eng)
            eng.tensor_scalar(half_var[:], mv[:, 1:2], EPS, -0.5, ALU.add, ALU.mult).then_inc(root_sem, 1)
            eng.wait_ge(root_sem, count + 1)
            plain(eng)
            eng.tensor_scalar(r[:, 0:1].bitcast(I32), half_var[:].bitcast(I32), -0.5, RSQRT_SEED,
                              ALU.mult, ALU.add).then_inc(root_sem, 1)
            for k in range(NEWTON):
                eng.wait_ge(root_sem, count + 2 * k + 2)
                plain(eng)
                eng.tensor_scalar(a[:], r[:, k:k + 1], r[:, k:k + 1], half_var[:], ALU.mult,
                                  ALU.mult).then_inc(root_sem, 1)
                eng.wait_ge(root_sem, count + 2 * k + 3)
                plain(eng)
                eng.tensor_scalar(r[:, k + 1:k + 2], a[:], 1.5, r[:, k:k + 1], ALU.add, ALU.mult).then_inc(root_sem, 1)
            eng.wait_ge(root_sem, count + LN_OPS)
            wait(eng, *dst_free)
            plain(eng)
            eng.tensor_scalar(dst, src, mv[:, 0:1], r[:, NEWTON:NEWTON + 1], ALU.subtract,
                               ALU.mult).then_inc(done_sem, 1)

        def residual_x2(eng, g, x2_free):
            normalise(eng, "y", y_norm[:], y[:], g, y_aggr, y_root, y_normed, (x2_ready, g))
            eng.wait_ge(y_normed, g + 1)
            eng.wait_ge(x_res_in, 16 * (g + 1))
            wait(eng, x2_normed, g)
            wait(eng, *x2_free)
            eng.tensor_tensor(x2[:], x_res[:], y_norm[:], ALU.add).then_inc(x2_ready, 1)

        def residual_out(eng, g, source):
            normalise(eng, "z", z_norm[:], z[:], g, z_aggr, z_root, z_normed, (out_ready, g))
            eng.wait_ge(z_normed, g + 1)
            if source is x2_keep:
                eng.wait_ge(x2_kept, g - KEPT_FROM + 1)
            wait(eng, out_stored, 16 * g)
            eng.tensor_tensor(out_sb[:], source[:], z_norm[:], ALU.add).then_inc(out_ready, 1)

        def normalise_x2(eng, g):
            normalise(eng, "x2", x2_norm[:], x2[:], g, x2_aggr, x2_root, x2_normed, (mixed_ready, 2 * KT * g))

        def g_early(g):
            return isinstance(g, int) and g < HEAD_LEAD

        def xh_load(g):
            if g_early(g):
                return (x_res if g % 2 else xh), (xh_odd_in if g % 2 else xh_in), 16 * (g // 2 + 1)
            return xh, xh_in, 16 * (g - HEAD_LEAD // 2 + 1)

        stat_steps = {"xh": (xh, xh_ready, xh_stats, xh_aggr), "y": (y, y_normed, y_stats, y_aggr),
                      "x2": (x2, x2_normed, x2_stats, x2_aggr), "z": (z, z_normed, z_stats, z_aggr)}

        x_rows = x.rearrange("(g p) c -> g p c", p=P)
        out_rows = out.rearrange("(g p) c -> g p c", p=P)
        o_rows = o_dram.rearrange("(g p) c -> g p c", p=P)
        o_heads = o_dram.rearrange("(b i p) (h d) -> b h p i d", b=B, p=P, d=D)

        block = ctx.enter_context(nc.Block())

        @block.sync
        def _(sp):

            def load_head(g):
                wait(sp, xh_ready, g - 1 if g_early(g) else g)
                buffer, loaded, _ = xh_load(g)
                sp.dma_start(buffer[:], x_rows[g]).then_inc(loaded, 16)

            def load_residual(g):
                wait(sp, x2_ready, g)
                sp.dma_start(x_res[:], x_rows[g]).then_inc(x_res_in, 16)

            def load_outputs(g):
                wait(sp, y_stats, g)
                sp.dma_start(o_cur[:], o_rows[g]).then_inc(o_cur_in, 16)

            def store_out(g):
                sp.wait_ge(out_ready, g + 1)
                sp.dma_start(out_rows[g], out_sb[:]).then_inc(out_stored, 16)

            def spread_qk(h):
                rows = slice(D * h, D * h + D)
                sp.dma_start(q_pair[h][0:D, :], q_stage[rows, 0, :]).then_inc(qk_in[h], 16)
                sp.dma_start(q_pair[h][D:P, :], q_stage[rows, 1, :]).then_inc(qk_in[h], 16)
                sp.dma_start(k_twice[h][0:D, :, :], k_stage[rows, :, :]).then_inc(qk_in[h], 16)
                sp.dma_start(k_twice[h][D:P, :, :], k_stage[rows, :, :]).then_inc(qk_in[h], 16)

            def spread_v(h):
                sp.dma_start(v_head[h][:].rearrange("p i (a d) -> p i a d", a=2),
                             v_stage[:, :, h, :, :]).then_inc(v_in[h], 16)

            load_head(0)
            load_head(1)
            sp.dma_start(w_f32[:], wqkv.rearrange("m (k p) n -> p m k n", p=P)).then_inc(weights_in, 16)
            sp.dma_start(tab_sb[:], table.rearrange("(o r) h -> o r h", o=1).to_broadcast([P, NBUCKET, H])
                         ).then_inc(table_in, 16)
            for dst, src in ((wp_sb, wp), (wr_sb, w_r), (wk_sb, w_k), (wv_sb, w_v)):
                sp.dma_start(dst[:], src.rearrange("(k p) n -> p k n", p=P)).then_inc(small_in, 16)
            sp.dma_start(bp_sb[:], bp.rearrange("(o c) -> o c", o=1).to_broadcast([P, C])).then_inc(small_in, 16)
            for m, mu in enumerate((mu_r, mu_k)):
                sp.dma_start(mu_sb[:, m, :], mu.rearrange("(k p) -> p k", p=P),
                             allow_slow_non_contiguous=True).then_inc(small_in, 16)
            for g in range(2, HEAD_LEAD):
                load_head(g)

            sp.wait_ge(vec_setup, 7)
            sp.dma_start(band_dram.rearrange("h (p j) -> p h j", p=P), band_src[:]).then_inc(band_out, 16)
            sp.wait_ge(band_out, 16)
            shifted = band_dram[:, P - 1:P - 1 + P * (ROW - 1)].rearrange("h (p j) -> p h j", j=ROW - 1)
            sp.dma_start(band[:], shifted[:, :, 0:WIN]).then_inc(band_in, 16)

            for k in range(2):
                sp.wait_ge(misc_free[k], first.end[1 + k])
            for h in range(2):
                spread_qk(h)
                spread_v(h)

            for seg in segments:
                def body(n, seg=seg):
                    if seg.front:
                        load_outputs(n - TAIL_LAG)
                    if seg.head:
                        load_head(n + HEAD_LEAD)
                    if seg.lo > TAIL_LAG + 1:
                        store_out(n - TAIL_LAG - 2)
                    for h in range(2):
                        if seg.next:
                            if h == 0:
                                evacuated(sp, seg.task(n, "k0"))
                                plain(sp)
                                evacuated(sp, seg.task(n, "k1"))
                                plain(sp)
                            sp.wait_ge(scored, UNITS * n + NB * (h + 1))
                            spread_qk(h)
                            if h == 0:
                                evacuated(sp, seg.task(n, "v0"))
                                plain(sp)
                                evacuated(sp, seg.task(n, "v1"))
                                plain(sp)
                            sp.wait_ge(pv_done, UNITS * n + NB * (h + 1))
                            spread_v(h)
                        if h == 0 and seg.front:
                            load_residual(n - TAIL_LAG)
                rolled(sp, seg.lo, seg.hi, body)

            def last_tails(g):
                load_outputs(g + 1)
                load_residual(g + 1)
                store_out(g - 1)
            for h in range(2):
                sp.wait_ge(o_stored[h], 16 * N)
            load_outputs(G - TAIL_LAG)
            store_out(G - TAIL_LAG - 2)
            load_residual(G - TAIL_LAG)
            rolled(sp, G - TAIL_LAG, G - 1, last_tails)
            store_out(G - 2)
            store_out(G - 1)
            sp.wait_ge(out_stored, 16 * G)

        @block.tensor
        def _(pe):
            def misc_open(task):
                wait(pe, misc_free[task.bank], task.opens)
                return misc_banks[task.bank]

            def head_transpose(g, task):
                pe.wait_ge(xh_ready, g + 1)
                misc = misc_open(task)
                for k in range(KT):
                    last = pe.transpose(misc[:, k * P:(k + 1) * P], xh_norm[:, k * P:(k + 1) * P], ident[:])
                last.then_inc(misc_full, 1)

            def project_qk(which, half, pair, ring, task):
                misc = misc_open(task)
                step = 0
                for k in range(KT):
                    for w, a in ((0, 0), (1, 0), (0, 1)):
                        last = pe.matmul(misc[:], w_split[:, w, which, k, bass.ds(pair, P)],
                                         xT[:, a, k, bass.ds(ring + half * 512, 512)],
                                         start=step == 0, stop=step == 3 * KT - 1)
                        step += 1
                last.then_inc(misc_full, 1)

            def project_v(half, pair, ring, task):
                misc = misc_open(task)
                for i in range(4):
                    step = 0
                    for k in range(KT):
                        for w, a in ((0, 0), (1, 0), (0, 1)):
                            last = pe.matmul(misc[:, i * P:(i + 1) * P],
                                             xT[:, a, k, bass.ds(ring + (half * 4 + i) * P, P)],
                                             w_split[:, w, 2, k, bass.ds(pair, P)],
                                             start=step == 0, stop=step == 3 * KT - 1)
                            step += 1
                last.then_inc(misc_full, 1)

            def next_task(name, pair, ring, task):
                if name[0] == "v":
                    project_v(int(name[1]), pair, ring, task)
                else:
                    project_qk("qk".index(name[0]), int(name[1]), pair, ring, task)

            def tail_task(name, g, tasks, n):
                task = tasks.task(n, name)
                if name in ("ot0", "ot1"):
                    half = int(name[2])
                    if half == 0:
                        pe.wait_ge(o_cur_in, 16 * (g + 1))
                    misc = misc_open(task)
                    for j in range(4):
                        c = half * 4 + j
                        last = pe.transpose(misc[:, j * P:(j + 1) * P], o_cur[:, c * P:(c + 1) * P], ident[:])
                elif name == "proj":
                    pe.wait_ge(vec_setup, 8)
                    evacuated(pe, tasks.task(n, "ot1"))
                    misc = misc_open(task)
                    for c in range(H * D // P):
                        last = pe.matmul(misc[:, 0:C], oT[:, c, :], wp_sb[:, c, :], start=c == 0,
                                         stop=c == H * D // P - 1)
                elif name == "x2t":
                    pe.wait_ge(x2_normed, g + 1)
                    misc = misc_open(task)
                    for k in range(KT):
                        last = pe.transpose(misc[:, k * P:(k + 1) * P], x2_norm[:, k * P:(k + 1) * P], ident[:])
                elif name == "rk":
                    pe.wait_ge(mixed_ready, 2 * KT * (g + 1))
                    misc = misc_open(task)
                    for k in range(KT):
                        pe.matmul(misc[:, 0:C], mixed[:, 0, k, :], wr_sb[:, k, :], start=k == 0, stop=k == KT - 1)
                    for m in range(KT):
                        for k in range(KT):
                            last = pe.matmul(misc[:, C + m * P:C + (m + 1) * P], wk_sb[:, k, m * P:(m + 1) * P],
                                             mixed[:, 1, k, :], start=k == 0, stop=k == KT - 1)
                else:
                    pe.wait_ge(k_act_ready, g + 1)
                    misc = misc_open(task)
                    for k in range(KT):
                        last = pe.matmul(misc[:, 0:C], k_act[:, k, :], wv_sb[:, k, :], start=k == 0,
                                         stop=k == KT - 1)
                last.then_inc(misc_full, 1)

            def score(n, u):
                (h, i), unit = head_block(u), UNITS * n + u
                if u % NB == 0:
                    pe.wait_ge(qk_in[h], 64 * (n + 1 + u // UNITS))
                wait(pe, exp_done, unit - 1)
                for c in range((i + 4) // 4):
                    cols = min(512, (i + 1) * P - c * 512)
                    for a in range(2):
                        last = pe.matmul(scores[u % 2][:, c * 512:c * 512 + cols], q_pair[h][:, i * P:(i + 1) * P],
                                         k_twice[h][:, a, c * 512:c * 512 + cols], start=a == 0, stop=a == 1)
                last.then_inc(scored, 1)

            def transpose_probs(n, u, some):
                pe.wait_ge(exp_done, UNITS * n + u + 1)
                for c, blocks in chunks(head_block(u)[1])[some]:
                    k = CHUNK0[u] + c
                    wait(pe, lo_done, CHUNKS * n + k - 1)
                    for j in range(blocks):
                        s = 4 * c + j
                        last = pe.transpose(probsT_ps[k % 2][:, j, :], probs[:, u % 2, s * P:(s + 1) * P], ident[:])
                    last.then_inc(transposed, 1)

            def weigh_values(n, u):
                h, i = head_block(u)
                if u % NB == 0:
                    pe.wait_ge(v_in[h], 16 * (n + 1))
                pe.wait_ge(lo_done, CHUNKS * n + chunks_before(u + 1))
                wait(pe, parts_ready, UNITS * n + u)
                for s in range(i + 1):
                    for a in range(2):
                        last = pe.matmul(o_ps[:, 0:2 * D], probsT[:, u % 2, a, s, :], v_head[h][:, s, :],
                                         start=s == 0 and a == 0, stop=s == i and a == 1)
                last.then_inc(pv_done, 1)

            pe.wait_ge(ident_ready, 1)
            rolled(pe, 0, HEAD_LEAD, lambda g: head_transpose(g, Task(0, g, g)))
            pe.wait_ge(split_lo, 3)
            for name in NEXT_TASKS:
                next_task(name, 0, 0, first.task(0, name))
            score(0, 0)
            score(0, 1)
            pe.wait_ge(small_in, 16 * 7)
            for seg in segments:
                def body(n, seg=seg):
                    pair, ring = (n + 1) % NPAIR * P, (n + 1) // NPAIR % 2 * T
                    if not isinstance(n, int):
                        pair, ring = pe.snap(pair), pe.snap(ring)
                    for u in range(UNITS):
                        transpose_probs(n, u, FIRST_CHUNK)
                        if u + 2 < UNITS or seg.next:
                            score(n, u + 2)
                        if u % 2:
                            transpose_probs(n, u, SECOND_CHUNK)
                        name = seg.in_slot.get(u)
                        if name in NEXT_TASKS:
                            next_task(name, pair, ring, seg.task(n, name))
                        elif name in FRONT_TASKS or name in BACK_TASKS:
                            tail_task(name, seg.tail_block(n, name), seg, n)
                        elif name in HEAD_TASKS:
                            head_transpose(n + HEAD_LEAD, seg.task(n, name))
                        if u > 0 or not isinstance(n, int) or n > 0:
                            weigh_values(n, u - 1)
                rolled(pe, seg.lo, seg.hi, body)
            weigh_values(N - 1, UNITS - 1)

            def last_tails(g):
                for name in LAST_ORDER:
                    tail_task(name, g - 1 if name in BACK_TASKS else g + 1, closing, g)
            for name in FRONT_TASKS:
                tail_task(name, G - TAIL_LAG, lead, G - TAIL_LAG)
            rolled(pe, G - TAIL_LAG, G - 1, last_tails)
            for g in (G - 1, G):
                for name in BACK_TASKS:
                    tail_task(name, g - 1, final, g)

        @block.scalar
        def _(act):
            def evacuate_high(dst, src, task):
                act.wait_ge(misc_full, task.full)
                nc.scalar.copy(dst, src).then_inc(misc_hi, 1)

            def head_high(g, task):
                misc = misc_banks[task.bank]
                at = act.snap(g % (RING // P) * P) if not isinstance(g, int) else g % (RING // P) * P
                evacuate_high(xT[:, 0, :, bass.ds(at, P)], misc[:, 0:C].rearrange("p (k t) -> p k t", k=KT), task)

            def next_high(name, pairs_before, task):
                misc = misc_banks[task.bank]
                half = int(name[1])
                if name == "q0":
                    wait(act, qk_in[1], 64 * pairs_before)
                if name == "v0":
                    wait(act, v_in[1], 16 * pairs_before)
                if name[0] == "v":
                    evacuate_high(v_stage[:, 4 * half:4 * half + 4, :, 0, :],
                                  misc[:].rearrange("p (i h d) -> p i h d", i=4, h=2), task)
                else:
                    stage = q_stage if name[0] == "q" else k_stage
                    evacuate_high(stage[:, 0, half * 512:(half + 1) * 512], misc[:], task)

            def tail_step(name, g, task):
                misc, freed = (misc_banks[task.bank], misc_free[task.bank]) if task else (None, None)
                if name in ("ot0", "ot1"):
                    half = int(name[2])
                    act.wait_ge(misc_full, task.full)
                    nc.scalar.copy(oT[:, half * 4:half * 4 + 4, :],
                                   misc[:].rearrange("p (c t) -> p c t", c=4)).then_inc(freed, 1)
                elif name == "x2t":
                    act.wait_ge(misc_full, task.full)
                    act.wait_ge(carried, KT * (g + 1))
                    nc.scalar.copy(x2T[:, :, 1:P + 1],
                                   misc[:, 0:C].rearrange("p (k t) -> p k t", k=KT)).then_inc(freed, 1)
                elif name == "rk":
                    act.wait_ge(misc_full, task.full)
                    nc.scalar.activation(gate_exp[:], misc[:, 0:C], ACT.Exp, scale=-1.0).then_inc(gate_exped, 1)
                    nc.scalar.activation(k_relu[:], misc[:, C:2 * C].rearrange("p (k t) -> p k t", k=KT),
                                         ACT.Relu).then_inc(freed, 1)

            def exponential(n, u):
                unit, i = UNITS * n + u, head_block(u)[1]
                act.wait_ge(bias_ready, unit + 1)
                wait(act, transposed, CHUNKS * n + chunks_before(u - 1))
                wait(act, inv_ready, unit - 3)
                cols = (i + 1) * P
                nc.scalar.activation(probs[:, u % 2, 0:cols], scores[u % 2][:, 0:cols], ACT.Exp,
                                     bias=exp_bias[:, u % 4:u % 4 + 1], scale=score_unit[:],
                                     accum_out=row_sum[:, u % 4:u % 4 + 1]).then_inc(exp_done, 1)

            def high_parts(n, u, some):
                for c, blocks in chunks(head_block(u)[1])[some]:
                    k = CHUNKS * n + CHUNK0[u] + c
                    act.wait_ge(transposed, k + 1)
                    if c == 0:
                        wait(act, pv_done, UNITS * n + u - 1)
                    nc.scalar.copy(probsT[:, u % 2, 0, 4 * c:4 * c + blocks, :],
                                   probsT_ps[(CHUNK0[u] + c) % 2][:, 0:blocks, :]).then_inc(hi_done, 1)

            def scale_output(n, u):
                unit = UNITS * n + u
                act.wait_ge(pv_done, unit + 1)
                act.wait_ge(inv_ready, unit + 1)
                wait(act, o_added, unit - 3)
                nc.scalar.activation(o_parts[:, u % 4, :], o_ps[:, 0:2 * D], ACT.Copy,
                                     scale=inv_sum[:, u % 4:u % 4 + 1]).then_inc(parts_ready, 1)

            rolled(act, 0, HEAD_LEAD, lambda g: head_high(g, Task(0, g, g)))
            for name in NEXT_TASKS:
                next_high(name, 0, first.task(0, name))
            exponential(0, 0)
            for seg in segments:
                def body(n, seg=seg):
                    for u in range(UNITS):
                        if u > 1 or not isinstance(n, int) or n > 0:
                            scale_output(n, u - 2)
                        high_parts(n, u, FIRST_CHUNK)
                        if u + 1 < UNITS or seg.next:
                            exponential(n, u + 1)
                        if u % 2:
                            high_parts(n, u, SECOND_CHUNK)
                        name = seg.in_slot.get(u)
                        if name in NEXT_TASKS:
                            next_high(name, n + 1, seg.task(n, name))
                        elif name in FRONT_TASKS or name in BACK_TASKS:
                            tail_step(name, seg.tail_block(n, name), seg.task(n, name))
                        elif name in HEAD_TASKS:
                            head_high(n + HEAD_LEAD, seg.task(n, name))
                rolled(act, seg.lo, seg.hi, body)
            scale_output(N - 1, UNITS - 2)
            scale_output(N - 1, UNITS - 1)

            def last_tails(g):
                for name in LAST_ORDER:
                    tail_step(name, g - 1 if name in BACK_TASKS else g + 1, closing.task(g, name))
            for name in FRONT_TASKS:
                tail_step(name, G - TAIL_LAG, lead.task(G - TAIL_LAG, name))
            rolled(act, G - TAIL_LAG, G - 1, last_tails)
            for g in (G - 1, G):
                for name in BACK_TASKS:
                    tail_step(name, g - 1, final.task(g, name))

        @block.vector
        def _(dve):
            def statistics(name, g, task=None):
                src, _, stats = stat_steps[name][:3]
                if name == "xh":
                    src, loaded, value = xh_load(g)
                    dve.wait_ge(loaded, value)
                    if g_early(g):
                        wait(dve, xh_aggr, g)
                elif name == "x2":
                    dve.wait_ge(x2_ready, g + 1)
                else:
                    evacuated(dve, task)
                dve.bn_stats(ln_bufs[name][0][:], src[:]).then_inc(stats, 1)

            def aggregate(name, g):
                bn, mv = ln_bufs[name][:2]
                _, used, stats, aggr = stat_steps[name]
                dve.wait_ge(stats, g + 1)
                wait(dve, used, g)
                plain(dve)
                dve.bn_aggr(mv[:], bn[:]).then_inc(aggr, 1)

            def evacuate_low(dst, src, high, hi_count, task):
                dve.wait_ge(misc_hi, hi_count)
                dve.tensor_tensor(dst, src, high, ALU.subtract).then_inc(misc_free[task.bank], 1)

            def head_low(g, hi_count, task):
                misc = misc_banks[task.bank]
                at = dve.snap(g % (RING // P) * P) if not isinstance(g, int) else g % (RING // P) * P
                evacuate_low(xT[:, 1, :, bass.ds(at, P)], misc[:, 0:C].rearrange("p (k t) -> p k t", k=KT),
                             xT[:, 0, :, bass.ds(at, P)], hi_count, task)

            def next_low(name, hi_count, task):
                misc = misc_banks[task.bank]
                half = int(name[1])
                if name[0] == "v":
                    evacuate_low(v_stage[:, 4 * half:4 * half + 4, :, 1, :],
                                 misc[:].rearrange("p (i h d) -> p i h d", i=4, h=2),
                                 v_stage[:, 4 * half:4 * half + 4, :, 0, :], hi_count, task)
                else:
                    stage = q_stage if name[0] == "q" else k_stage
                    cols = slice(half * 512, (half + 1) * 512)
                    evacuate_low(stage[:, 1, cols], misc[:], stage[:, 0, cols], hi_count, task)

            def tail_step(name, g, task):
                misc, freed = (misc_banks[task.bank], misc_free[task.bank]) if task else (None, None)
                if name == "proj":
                    dve.wait_ge(misc_full, task.full)
                    wait(dve, y_normed, g)
                    dve.tensor_tensor(y[:], misc[:, 0:C], bp_sb[:], ALU.add).then_inc(freed, 1)
                    statistics("y", g, task)
                elif name == "mix":
                    dve.wait_ge(delta_ready, g + 1)
                    for m in range(2):
                        for k in range(KT):
                            dve.scalar_tensor_tensor(mixed[:, m, k, :], delta[:, k, :], mu_sb[:, m, k:k + 1],
                                                     x2T[:, k, 0:P], ALU.mult, ALU.add).then_inc(mixed_ready, 1)
                elif name in ("gate0", "gate1"):
                    cols = slice(int(name[4]) * P, int(name[4]) * P + P)
                    dve.wait_ge(den_ready, g + 1)
                    wait(dve, z_stats, g)
                    dve.reciprocal(gate[:, cols], gate_den[:, cols]).then_inc(gate_ready, 1)
                elif name == "ffn":
                    dve.wait_ge(misc_full, task.full)
                    dve.wait_ge(gate_ready, 2 * (g + 1))
                    wait(dve, z_normed, g)
                    dve.tensor_tensor(z[:], misc[:, 0:C], gate[:], ALU.mult).then_inc(freed, 1)

            def bias_and_maximum(n, u):
                (h, i), unit = head_block(u), UNITS * n + u
                cols = (i + 1) * P
                pair_count = n + 1 + u // UNITS
                if u % NB == 0:
                    dve.wait_ge(bias_row_in[h], pair_count)
                dve.wait_ge(scored, unit + 1)
                plain(dve)
                dve.tensor_tensor_reduce(out=scores[u % 2][:, 0:cols], in0=scores[u % 2][:, 0:cols],
                                         in1=bias_row[h][:, T - cols:T], scale=1.0, scalar=-3.4e38, op0=ALU.add,
                                         op1=ALU.max, accum_out=row_max[:, u % 4:u % 4 + 1]).then_inc(max_ready, 1)

            def exponential_bias(n, u):
                unit = UNITS * n + u
                dve.wait_ge(max_ready, unit + 1)
                wait(dve, exp_done, unit - 3)
                dve.tensor_scalar(exp_bias[:, u % 4:u % 4 + 1], row_max[:, u % 4:u % 4 + 1], neg_unit[:, 0:1],
                                  P_SHIFT, ALU.mult, ALU.add).then_inc(bias_ready, 1)

            def low_parts(n, u, some):
                for c, blocks in chunks(head_block(u)[1])[some]:
                    k = CHUNKS * n + CHUNK0[u] + c
                    dve.wait_ge(hi_done, k + 1)
                    dve.tensor_tensor(probsT[:, u % 2, 1, 4 * c:4 * c + blocks, :],
                                      probsT_ps[(CHUNK0[u] + c) % 2][:, 0:blocks, :],
                                      probsT[:, u % 2, 0, 4 * c:4 * c + blocks, :], ALU.subtract).then_inc(lo_done, 1)

            def invert_sum(n, u):
                unit = UNITS * n + u
                dve.wait_ge(exp_done, unit + 1)
                wait(dve, parts_ready, unit - 3)
                dve.reciprocal(inv_sum[:, u % 4:u % 4 + 1], row_sum[:, u % 4:u % 4 + 1]).then_inc(inv_ready, 1)

            def find_top():
                dve.wait_ge(weights_in, 16)
                for m in range(3):
                    last = dve.tensor_reduce(top[:, m:m + 1], w_f32[:, m, :, :], AX.XY, ALU.max,
                                             apply_absolute_value=True)
                last.then_inc(top_ready, 1)

            def make_scales():
                dve.wait_ge(top_reduced, 1)
                dve.tensor_scalar(top_all[:], top_all[:], 2.0 ** -40, None, ALU.max).then_inc(vec_setup, 1)
                dve.wait_ge(vec_setup, 1)
                dve.tensor_scalar(pow2[:].bitcast(I32), top_all[:].bitcast(I32), 0x7F800000, None,
                                  ALU.bitwise_and).then_inc(vec_setup, 1)
                dve.wait_ge(vec_setup, 2)
                dve.reciprocal(inv2[:], pow2[:]).then_inc(vec_setup, 1)
                dve.wait_ge(vec_setup, 3)
                dve.tensor_scalar(w_scale[:], inv2[:], W_TOP, None, ALU.mult)
                dve.tensor_scalar(score_unit[:], pow2[:, 0:1], pow2[:, 1:2], D ** -0.5 / W_TOP ** 2,
                                  ALU.mult, ALU.mult)
                dve.tensor_scalar(neg_unit[:], pow2[:, 0:1], pow2[:, 1:2], -D ** -0.5 / W_TOP ** 2,
                                  ALU.mult, ALU.mult)
                dve.tensor_scalar(band_unit[:], inv2[:, 0:1], inv2[:, 1:2], D ** 0.5 * W_TOP ** 2,
                                  ALU.mult, ALU.mult).then_inc(vec_setup, 1)
                dve.wait_ge(vec_setup, 4)

            def split_weights(m):
                dve.tensor_scalar(w_split[:, 0, m], w_f32[:, m], w_scale[:, m:m + 1], None,
                                  ALU.mult).then_inc(split_hi, 1)
                dve.wait_ge(split_hi, m + 1)
                dve.scalar_tensor_tensor(w_split[:, 1, m], w_f32[:, m], w_scale[:, m:m + 1], w_split[:, 0, m],
                                         ALU.mult, ALU.subtract).then_inc(split_lo, 1)

            def make_band():
                dve.wait_ge(table_in, 16)
                dve.memset(band_src[:, :, 0:P], 0.0)
                dve.memset(band_src[:, :, WIN:ROW], MASKED).then_inc(vec_setup, 1)
                dve.tensor_tensor(band_src[:, :, P:WIN], tab_sb[:, 1:1 + MAX_REL, :].rearrange("p r h -> p h r"),
                                  tab_sb[:, 0:1, :].rearrange("p r h -> p h r").to_broadcast([P, H, MAX_REL]),
                                  ALU.subtract).then_inc(vec_setup, 1)
                dve.wait_ge(vec_setup, 6)
                dve.tensor_scalar(band_src[:, :, P:WIN], band_src[:, :, P:WIN], band_unit[:, 0:1], None,
                                  ALU.mult).then_inc(vec_setup, 1)

            def scale_output_weights():
                dve.wait_ge(small_in, 16 * 7)
                dve.tensor_scalar(wp_sb[:], wp_sb[:], pow2[:, 2:3], 1.0 / W_TOP, ALU.mult,
                                  ALU.mult).then_inc(vec_setup, 1)

            between = {3: find_top, 4: make_scales, 5: make_band, 6: lambda: split_weights(0),
                       7: lambda: split_weights(1), 8: lambda: split_weights(2)}
            for g in range(HEAD_LEAD):
                statistics("xh", g)
                aggregate("xh", g)
                if g > 0:
                    head_low(g - 1, g, Task(0, g - 1, g - 1))
                if g in between:
                    between[g]()
            head_low(HEAD_LEAD - 1, HEAD_LEAD, Task(0, HEAD_LEAD - 1, HEAD_LEAD - 1))
            for k, name in enumerate(NEXT_TASKS):
                next_low(name, HEAD_LEAD + k + 1, first.task(0, name))
            for u in range(2):
                bias_and_maximum(0, u)
                exponential_bias(0, u)
            scale_output_weights()

            two_part = {**NEXT_TASKS, **HEAD_TASKS}
            hi_base = HEAD_LEAD + len(NEXT_TASKS)
            for seg in segments:
                split = [name for name in seg.order if name in two_part]

                def body(n, seg=seg, split=split, hi_base=hi_base):
                    for u in range(UNITS):
                        low_parts(n, u, FIRST_CHUNK)
                        stat = VEC_STATS.get(u)
                        if stat and seg.has(stat):
                            statistics(stat, seg.step_block(n, stat), seg.task(n, "ffn") if stat == "z" else None)
                        if u + 2 < UNITS or seg.next:
                            bias_and_maximum(n, u + 2)
                        invert_sum(n, u)
                        stat = VEC_AGGR.get(u)
                        if stat and seg.has(stat):
                            aggregate(stat, seg.step_block(n, stat))
                        if u + 2 < UNITS or seg.next:
                            exponential_bias(n, u + 2)
                        if u % 2:
                            low_parts(n, u, SECOND_CHUNK)
                        name = seg.in_slot.get(u)
                        if name in split:
                            count = hi_base + len(split) * (n - seg.lo) + split.index(name) + 1
                            if name in NEXT_TASKS:
                                next_low(name, count, seg.task(n, name))
                            else:
                                head_low(n + HEAD_LEAD, count, seg.task(n, name))
                        elif name in ("proj", "ffn"):
                            tail_step(name, seg.tail_block(n, name), seg.task(n, name))
                        step = VEC_STEPS.get(u)
                        if step and seg.has(step):
                            tail_step(step, seg.tail_block(n, step), None)
                rolled(dve, seg.lo, seg.hi, body)
                hi_base += len(split) * (seg.hi - seg.lo)

            def make_x2(g, x2_free):
                aggregate("y", g)
                residual_x2(dve, g, x2_free)
                statistics("x2", g)
                aggregate("x2", g)

            def make_z(g, task):
                tail_step("gate0", g, None)
                tail_step("gate1", g, None)
                tail_step("ffn", g, task)
                statistics("z", g, task)
                aggregate("z", g)

            def last_tails(g, tasks=closing):
                tail_step("mix", g - 1, None)
                make_x2(g, (x2_kept, g - KEPT_FROM))
                make_z(g - 1, tasks.task(g, "ffn"))
                normalise_x2(dve, g)
                if tasks is closing:
                    tail_step("proj", g + 1, closing.task(g, "proj"))

            make_x2(KEPT_FROM, (out_ready, KEPT_FROM))
            tail_step("proj", KEPT_FROM + 1, lead.task(KEPT_FROM + 1, "proj"))
            normalise_x2(dve, KEPT_FROM)
            rolled(dve, G - TAIL_LAG, G - 1, last_tails)
            last_tails(G - 1, final)
            tail_step("mix", G - 1, None)
            make_z(G - 1, final.task(G, "ffn"))

        @block.gpsimd
        def _(pool):
            def add_parts(n, u):
                (h, i), unit = head_block(u), UNITS * n + u
                pool.wait_ge(parts_ready, unit + 1)
                if u % NB == 0:
                    wait(pool, o_stored[h], 16 * n if u >= 0 else 16 * (n - 1))
                pool.tensor_tensor(o_stage[h][:, i, :], o_parts[:, u % 4, 0:D], o_parts[:, u % 4, D:2 * D],
                                   ALU.add).then_inc(o_added, 1)

            def set_bias_row(n, h, pair):
                wait(pool, max_ready, UNITS * (n - 1) + NB * (h + 1))
                pool.tensor_copy(bias_row[h][:, T - WIN:T], band[:, bass.ds(2 * pair + h, 1), :].rearrange(
                    "p o j -> p (o j)")).then_inc(bias_row_in[h], 1)

            def store_head(n, h, b, pair):
                pool.wait_ge(o_added, UNITS * n + NB * (h + 1))
                pool.dma_start(o_heads[b, pair * 2 + h], o_stage[h][:]).then_inc(o_stored[h], 16)

            def tail_step(name, g):
                if name == "x2":
                    residual_x2(pool, g, (out_ready, g))
                elif name == "x2_norm":
                    normalise_x2(pool, g)
                    tail_step("carry", g)
                elif name == "carry":
                    wait(pool, mixed_ready, 2 * KT * g)
                    for k in range(KT):
                        pool.tensor_tensor(x2T[:, k, 0:1], x2T[:, k, P:P + 1], keep_carry[:, bass.ds(g, 1)],
                                           ALU.mult).then_inc(carried, 1)
                elif name == "delta":
                    pool.tensor_tensor(delta[:], x2T[:, :, 1:P + 1], x2T[:, :, 0:P],
                                       ALU.subtract).then_inc(delta_ready, 1)
                elif name == "act":
                    pool.wait_ge(gate_exped, g + 1)
                    wait(pool, gate_ready, 2 * g)
                    plain(pool)
                    pool.tensor_scalar(gate_den[:], gate_exp[:], 1.0, None, ALU.add).then_inc(den_ready, 1)
                    pool.tensor_tensor(k_act[:], k_relu[:], k_relu[:], ALU.mult).then_inc(k_act_ready, 1)
                elif name == "keep":
                    pool.wait_ge(x2_ready, g + 1)
                    pool.wait_ge(out_ready, g)
                    plain(pool)
                    pool.tensor_copy(x2_keep[:], x2[:]).then_inc(x2_kept, 1)
                else:
                    residual_out(pool, g, x2)

            pool.memset(ident[:], 0.0).then_inc(pool_setup, 1)
            pool.wait_ge(pool_setup, 1)
            pool.affine_select(out=ident[:], in_=ident[:], compare_op=ALU.not_equal, fill=1.0, base=0,
                               pattern=[[-1, P]], channel_multiplier=1).then_inc(ident_ready, 1)
            pool.memset(keep_carry[:], 1.0).then_inc(pool_setup, 1)
            pool.memset(x2T[:], 0.0).then_inc(pool_setup, 1)
            for h in range(2):
                pool.memset(bias_row[h][:, 0:T - WIN], 0.0).then_inc(pool_setup, 1)
            pool.wait_ge(pool_setup, 5)
            pool.memset(keep_carry[:].rearrange("p (b i) -> p b i", i=NB)[:, :, 0:1], 0.0).then_inc(pool_setup, 1)
            pool.wait_ge(pool_setup, 6)

            for g in range(HEAD_LEAD):
                normalise(pool, "xh", xh_norm[:], xh_load(g)[0][:], g, xh_aggr, xh_root, xh_ready, (misc_full, g))
                if g == 3:
                    pool.wait_ge(top_ready, 1)
                    pool.partition_all_reduce(top_all[:], top[:], P, bass.bass_isa.ReduceOp.max
                                              ).then_inc(top_reduced, 1)
            pool.wait_ge(band_in, 16)
            set_bias_row(0, 0, 0)
            set_bias_row(0, 1, 0)
            for seg in segments:
                def body(n, seg=seg):
                    g = n - TAIL_LAG
                    b, pair = (n // NPAIR, n % NPAIR) if isinstance(n, int) else (pool.snap(n // NPAIR),
                                                                                pool.snap(n % NPAIR))
                    next_pair = (n + 1) % NPAIR if isinstance(n, int) else pool.snap((n + 1) % NPAIR)
                    for u in range(UNITS):
                        if u > 1 or not isinstance(n, int) or n > 0:
                            add_parts(n, u - 2)
                        if u == 1 and (not isinstance(n, int) or n > 0):
                            if isinstance(n, int):
                                store_head(n - 1, 1, (n - 1) // NPAIR, (n - 1) % NPAIR)
                            else:
                                store_head(n - 1, 1, pool.snap((n - 1) // NPAIR), pool.snap((n - 1) % NPAIR))
                        if u == NB + 1:
                            store_head(n, 0, b, pair)
                            if seg.next:
                                set_bias_row(n + 1, 0, next_pair)
                        if u == 0 and (not isinstance(n, int) or n > 0):
                            set_bias_row(n, 1, pair)
                        step = POOL_STEPS.get(u)
                        if step == "head" and seg.head:
                            normalise(pool, "xh", xh_norm[:], xh[:], n + HEAD_LEAD, xh_aggr, xh_root, xh_ready,
                                      (misc_full, seg.counts[0] + seg.steps[0] * (n - seg.lo)))
                        elif step and step != "head" and seg.has(step):
                            if step == "delta":
                                evacuated(pool, seg.task(n, "x2t"))
                            if step == "act":
                                evacuated(pool, seg.task(n, "rk"))
                            tail_step(step, seg.tail_block(n, step))
                rolled(pool, seg.lo, seg.hi, body)
            add_parts(N - 1, UNITS - 2)
            add_parts(N - 1, UNITS - 1)
            store_head(N - 1, 1, B - 1, NPAIR - 1)

            def last_tails(g, tasks=closing):
                evacuated(pool, tasks.task(g, "x2t"))
                tail_step("delta", g - 1)
                tail_step("keep", g - 1)
                evacuated(pool, tasks.task(g, "rk"))
                tail_step("act", g - 1)
                if not isinstance(g, int) or g < G:
                    tail_step("carry", g)
                residual_out(pool, g - 1, x2_keep)
            tail_step("carry", KEPT_FROM)
            rolled(pool, G - TAIL_LAG, G - 1, last_tails)
            last_tails(G - 1, final)
            last_tails(G, final)


def kernel(**inputs):
    import numpy as np
    import concourse.bacc as bacc
    from concourse.bass_utils import run_bass_kernel_spmd

    a = {k.split("_", 1)[1]: np.asarray(v) for k, v in inputs.items()}
    heads_last = [a[f"attn_{w}"].transpose(1, 0, 2).reshape(C, H * D) for w in ("Wq", "Wk", "Wv")]
    arrays = {
        "x": a["attn_x"].reshape(B * T, C),
        "wqkv": np.stack(heads_last),
        "wp": a["attn_Wp"],
        "bp": a["attn_bp"],
        "table": a["attn_rel_table"],
        "w_r": a["ffn_W_r"].T,
        "w_k": a["ffn_W_k"].T,
        "w_v": a["ffn_W_v"].T,
        "mu_r": a["ffn_mu_r"],
        "mu_k": a["ffn_mu_k"],
    }
    arrays = {k: np.ascontiguousarray(v) for k, v in arrays.items()}
    nc = bacc.Bacc("TRN2", target_bir_lowering=False, num_devices=1)
    args = [nc.dram_tensor(k, v.shape, mybir.dt.from_np(v.dtype), kind="ExternalInput").ap()
            for k, v in arrays.items()]
    out = nc.dram_tensor("out", [B * T, C], F32, kind="ExternalOutput").ap()
    build(nc, *args, out)
    r = run_bass_kernel_spmd(nc, [arrays], core_ids=[0])
    return r.results[0]["out"].reshape(B, T, C)
```
